# Optimizing a Trainium2 kernel written in Bass

```python
import numpy as np
import jax
import jax.numpy as jnp

def _softmax(x, axis=-1):
    return jax.nn.softmax(x, axis=axis)

def _gelu(x):
    return jax.nn.gelu(x, approximate=True)

def _silu(x):
    return jax.nn.silu(x)

def _sigmoid(x):
    return jax.nn.sigmoid(x)

def _layernorm(x, axis=-1, eps=1e-05):
    m = jnp.mean(x, axis=axis, keepdims=True)
    v = jnp.var(x, axis=axis, keepdims=True)
    return (x - m) / jnp.sqrt(v + eps)

def _scatter_add(tgt, idx, src, axis=0):
    return tgt.at[idx].add(src)

def _segment_sum(src, seg, n):
    return jax.ops.segment_sum(src, seg, n)
kernel_name = 'mk_early_fusion_d1_tok_img512_r4_6033d2'

def setup_inputs(seed: int=0):
    np.random.seed(seed)
    _w = jnp.asarray

    def _rec_inputs():
        import jax
        import jax.numpy as jnp
        _rk = jax.random.key(seed)
        x = -0.000147625 + 0.999875 * jax.random.normal(jax.random.fold_in(_rk, 1), (64, 3, 224, 224), jnp.float32)
        txt = 0.00355565 + 0.408319 * jax.random.normal(jax.random.fold_in(_rk, 2), (64, 128, 128), jnp.float32)
        return (x, txt)
    x, txt = _rec_inputs()

    def _L0_tok_setup():
        import jax, jax.numpy as jnp
        import numpy as np
        N_PATCHES = 8
        PATCH = 28
        C = 3
        IN_D = C * PATCH * PATCH
        HID = 128
        SEQ = N_PATCHES * N_PATCHES + 1

        def _positional_embedding(seq_len, dim):
            i = np.arange(seq_len)[:, None].astype(np.float32)
            j = np.arange(dim)[None, :].astype(np.float32)
            ang = i / np.power(100000.0, j / dim)
            pe = np.where(j % 2 == 0, np.sin(ang), np.cos(ang))
            return jnp.asarray(pe, dtype=jnp.float32)
        key = jax.random.key(seed)
        k1, k2, k3, k4 = jax.random.split(key, 4)
        B = 64
        X = jax.random.normal(k1, (B, C, 224, 224), dtype=jnp.float32)
        bound = 1.0 / np.sqrt(IN_D)
        W = jax.random.uniform(k2, (HID, IN_D), minval=-bound, maxval=bound, dtype=jnp.float32)
        b = jax.random.uniform(k3, (HID,), minval=-bound, maxval=bound, dtype=jnp.float32)
        class_token = jax.random.uniform(k4, (1, HID), dtype=jnp.float32)
        pos_embed = _positional_embedding(SEQ, HID)
        return {'X': X, 'W': W, 'b': b, 'class_token': class_token, 'pos_embed': pos_embed}
    _L0_tok_all = _L0_tok_setup()
    _L0_tok_in = {k: v for k, v in _L0_tok_all.items() if k in ('W', 'b', 'class_token', 'pos_embed')}
    del _L0_tok_all

    def _L0_attn_setup():
        import jax, jax.numpy as jnp
        import numpy as np
        NUM_HEADS = 8
        NUM_GROUPS = 32
        EPS = 0.0001

        def group_norm(x, scale, bias):
            b, l, c = x.shape
            xg = x.reshape(b, l, NUM_GROUPS, c // NUM_GROUPS)
            mean = jnp.mean(xg, axis=(1, 3), keepdims=True)
            var = jnp.var(xg, axis=(1, 3), keepdims=True)
            xg = (xg - mean) * jax.lax.rsqrt(var + EPS)
            return xg.reshape(b, l, c) * scale + bias
        key = jax.random.key(seed)
        ks = jax.random.split(key, 6)
        bs, L, C = (4, 256, 128)
        hf = C // NUM_HEADS
        x = jax.random.normal(ks[0], (bs, L, C), dtype=jnp.float32)
        W_qkv = jax.random.normal(ks[1], (C, C * 2), dtype=jnp.float32) * (1.0 / C)
        gn_qkv_scale = jnp.ones((C * 2,), dtype=jnp.float32)
        gn_qkv_bias = jnp.zeros((C * 2,), dtype=jnp.float32)
        rel_emb = jax.random.normal(ks[2], (hf * 2, 2 * L - 1), dtype=jnp.float32) * (1.0 / hf)
        gn_out_scale = jnp.ones((C,), dtype=jnp.float32)
        gn_out_bias = jnp.zeros((C,), dtype=jnp.float32)
        return {'x': x, 'W_qkv': W_qkv, 'gn_qkv_scale': gn_qkv_scale, 'gn_qkv_bias': gn_qkv_bias, 'rel_emb': rel_emb, 'gn_out_scale': gn_out_scale, 'gn_out_bias': gn_out_bias}
    _L0_attn_all = _L0_attn_setup()
    _L0_attn_in = {k: v for k, v in _L0_attn_all.items() if k in ('W_qkv', 'gn_qkv_scale', 'gn_qkv_bias', 'rel_emb', 'gn_out_scale', 'gn_out_bias')}
    del _L0_attn_all

    def _L0_ffn_setup():
        import jax, jax.numpy as jnp
        import numpy as np
        K = 2
        key = jax.random.key(seed)
        ks = jax.random.split(key, 6)
        B, T, d, E, dff = (2, 512, 128, 8, 512)
        x = jax.random.normal(ks[0], (B, T, d), dtype=jnp.float32)
        Wg = jax.random.normal(ks[1], (d, E), dtype=jnp.float32) * 0.02
        W1 = jax.random.normal(ks[2], (E, d, dff), dtype=jnp.float32) * 0.02
        b1 = jnp.zeros((E, dff), dtype=jnp.float32)
        W2 = jax.random.normal(ks[3], (E, dff, d), dtype=jnp.float32) * 0.02
        b2 = jnp.zeros((E, d), dtype=jnp.float32)
        return {'x': x, 'Wg': Wg, 'W1': W1, 'b1': b1, 'W2': W2, 'b2': b2}
    _L0_ffn_all = _L0_ffn_setup()
    _L0_ffn_in = {k: v for k, v in _L0_ffn_all.items() if k in ('Wg', 'W1', 'b1', 'W2', 'b2')}
    del _L0_ffn_all
    return {'x': x, 'txt': txt, 'L0_tok_W': _L0_tok_in['W'], 'L0_tok_b': _L0_tok_in['b'], 'L0_tok_class_token': _L0_tok_in['class_token'], 'L0_tok_pos_embed': _L0_tok_in['pos_embed'], 'L0_attn_W_qkv': _L0_attn_in['W_qkv'], 'L0_attn_gn_qkv_scale': _L0_attn_in['gn_qkv_scale'], 'L0_attn_gn_qkv_bias': _L0_attn_in['gn_qkv_bias'], 'L0_attn_rel_emb': _L0_attn_in['rel_emb'], 'L0_attn_gn_out_scale': _L0_attn_in['gn_out_scale'], 'L0_attn_gn_out_bias': _L0_attn_in['gn_out_bias'], 'L0_ffn_Wg': _L0_ffn_in['Wg'], 'L0_ffn_W1': _L0_ffn_in['W1'], 'L0_ffn_b1': _L0_ffn_in['b1'], 'L0_ffn_W2': _L0_ffn_in['W2'], 'L0_ffn_b2': _L0_ffn_in['b2']}

def reference(x, txt, L0_tok_W, L0_tok_b, L0_tok_class_token, L0_tok_pos_embed, L0_attn_W_qkv, L0_attn_gn_qkv_scale, L0_attn_gn_qkv_bias, L0_attn_rel_emb, L0_attn_gn_out_scale, L0_attn_gn_out_bias, L0_ffn_Wg, L0_ffn_W1, L0_ffn_b1, L0_ffn_W2, L0_ffn_b2):
    import jax
    import jax.numpy as jnp

    def _L0_tok_ref(X, W, b, class_token, pos_embed):
        import jax, jax.numpy as jnp
        import numpy as np
        N_PATCHES = 8
        PATCH = 28
        C = 3
        IN_D = C * PATCH * PATCH
        HID = 128
        SEQ = N_PATCHES * N_PATCHES + 1

        def _positional_embedding(seq_len, dim):
            i = np.arange(seq_len)[:, None].astype(np.float32)
            j = np.arange(dim)[None, :].astype(np.float32)
            ang = i / np.power(100000.0, j / dim)
            pe = np.where(j % 2 == 0, np.sin(ang), np.cos(ang))
            return jnp.asarray(pe, dtype=jnp.float32)
        B = X.shape[0]
        patches = X.reshape(B, C, N_PATCHES, PATCH, N_PATCHES, PATCH)
        patches = patches.transpose(0, 2, 4, 1, 3, 5).reshape(B, N_PATCHES * N_PATCHES, IN_D)
        tokens = jnp.einsum('bpi,hi->bph', patches, W) + b
        cls = jnp.broadcast_to(class_token[None, :, :], (B, 1, HID))
        tokens = jnp.concatenate([cls, tokens], axis=1)
        return tokens * pos_embed[None, :, :]

    def _L0_attn_ref(x, W_qkv, gn_qkv_scale, gn_qkv_bias, rel_emb, gn_out_scale, gn_out_bias):
        import jax, jax.numpy as jnp
        import numpy as np
        NUM_HEADS = 8
        NUM_GROUPS = 32
        EPS = 0.0001

        def group_norm(x, scale, bias):
            b, l, c = x.shape
            xg = x.reshape(b, l, NUM_GROUPS, c // NUM_GROUPS)
            mean = jnp.mean(xg, axis=(1, 3), keepdims=True)
            var = jnp.var(xg, axis=(1, 3), keepdims=True)
            xg = (xg - mean) * jax.lax.rsqrt(var + EPS)
            return xg.reshape(b, l, c) * scale + bias
        bs, L, C = x.shape
        hf = C // NUM_HEADS
        qkv = x @ W_qkv
        qkv = group_norm(qkv, gn_qkv_scale, gn_qkv_bias)
        qkv = qkv.reshape(bs, L, NUM_HEADS, hf * 2).transpose((0, 2, 3, 1))
        q = qkv[:, :, :hf // 2]
        k = qkv[:, :, hf // 2:hf]
        v = qkv[:, :, hf:]
        rel_idx = jnp.arange(L)[:, None] - jnp.arange(L)[None, :] + (L - 1)
        rpe = rel_emb[:, rel_idx]
        rpe_q = rpe[:hf // 2]
        rpe_k = rpe[hf // 2:hf]
        rpe_v = rpe[hf:]
        logits = jnp.einsum('bhdi,bhdj->bhij', q, k) + jnp.einsum('bhdi,dij->bhij', q, rpe_k) + jnp.einsum('bhdi,dij->bhij', k, rpe_q)
        attn = jax.nn.softmax(logits, axis=3).astype(jnp.float32)
        wv = jnp.einsum('bhij,bhdj->bhdi', attn, v)
        wve = jnp.einsum('bhij,dij->bhdi', attn, rpe_v)
        out = (wv + wve).transpose((0, 3, 1, 2)).reshape(bs, L, C)
        return group_norm(out, gn_out_scale, gn_out_bias)

    def _L0_ffn_ref(x, Wg, W1, b1, W2, b2):
        import jax, jax.numpy as jnp
        import numpy as np
        K = 2
        logits = jnp.einsum('btd,de->bte', x, Wg)
        probs = jax.nn.softmax(logits, axis=-1)
        top_p, _top_i = jax.lax.top_k(probs, K)
        top_p = top_p / jnp.sum(top_p, axis=-1, keepdims=True)
        b2_sum = jnp.sum(b2, axis=0)
        out = jnp.zeros_like(x)
        for i in range(K):
            w_in = x * top_p[..., i:i + 1]
            h = jax.nn.gelu(jnp.einsum('btd,edf->ebtf', w_in, W1) + b1[:, None, None, :], approximate=False)
            out = out + jnp.einsum('ebtf,efd->btd', h, W2) + b2_sum
        return out
    h = _L0_tok_ref(x, L0_tok_W, L0_tok_b, L0_tok_class_token, L0_tok_pos_embed)
    h = jnp.concatenate([h, txt], axis=1)
    h = h + _L0_attn_ref(_layernorm(h, axis=-1), L0_attn_W_qkv, L0_attn_gn_qkv_scale, L0_attn_gn_qkv_bias, L0_attn_rel_emb, L0_attn_gn_out_scale, L0_attn_gn_out_bias)
    h = h + _L0_ffn_ref(_layernorm(h, axis=-1), L0_ffn_Wg, L0_ffn_W1, L0_ffn_b1, L0_ffn_W2, L0_ffn_b2)
    return h

_drawn_inputs = setup_inputs


def setup_inputs(seed=0):
    import zlib

    import numpy as np

    out = dict(_drawn_inputs(seed))
    spreads = {'L0_attn_gn_qkv_scale': (1.0, 0.2),
     'L0_attn_gn_qkv_bias': (0.0, 0.1),
     'L0_attn_gn_out_scale': (1.0, 0.2),
     'L0_attn_gn_out_bias': (0.0, 0.1),
     'L0_ffn_b1': (0.0, 0.1),
     'L0_ffn_b2': (0.0, 0.1)}
    factors = {}
    for name, (base, spread) in spreads.items():
        noise = np.random.default_rng([zlib.crc32(name.encode()), seed]).standard_normal(out[name].shape)
        drawn = base * np.exp(spread * noise) if base else spread * noise
        out[name] = jnp.asarray(drawn.astype(out[name].dtype))
    for name, factor in factors.items():
        out[name] = (out[name] * factor).astype(out[name].dtype)
    return out
```

```python
from contextlib import ExitStack

import concourse.bass as bass
from concourse import mybir

F32 = mybir.dt.float32
F32R = mybir.dt.float32r
ACT = mybir.ActivationFunctionType
ALU = mybir.AluOpType
AX = mybir.AxisListType.X

P = 128
B, C_IN, IMG = 64, 3, 224
NP_, PATCH = 8, 28
NPATCH = NP_ * NP_
ROWS = C_IN * PATCH
TXT = 128
L = 1 + NPATCH + TXT
PAIRS = B // 2
T2 = 2 * L
H, HD, DK = 8, 16, 8
BH = 2 * H
OCT = 25
LP = 8 * OCT
GRP = 4
NG = (OCT + GRP - 1) // GRP
JC = [(0, 128), (128, L - 128)]
E, FF = 8, 512
NF = E * FF // P
RING = 4
LAG = 3
GT = [(0, 97), (97, 97), (194, 96), (290, 96)]
LN_EPS, GN_EPS = 1e-5, 1e-4
NB0 = 4
NT0 = B // NB0

CO = {}
_at = 0
for _n, _w in (("ident", P), ("ones", P), ("g8", P), ("g4", P), ("mask_bh", BH), ("mask_r", 8), ("mask_q", 8),
               ("place", 112 + HD + 112)):
    CO[_n] = (_at, _w)
    _at += _w
NCONST = _at

SCHEDULE = (
    "txt c mean1 c c var1 c c proj c c gmean c gvar c c "
    "sel0 c sel1 c sel2 c sel3 c vt0 max0 c max1 c mrow c "
    "vt1 scores pv0 c c pv1 rel place c c omean c ovar c mean2 c c var2 c c gate c top c bcast c"
).split()


def attention_steps():
    return [s for s in SCHEDULE if s != "c"]


assert SCHEDULE.count("c") <= NF


def patch_embed(nc, x, w_tok, tok_scratch):
    with ExitStack() as ctx:
        sb = lambda n, s, d=F32: ctx.enter_context(nc.sbuf_tensor(n, s, d))
        sem = lambda n: ctx.enter_context(nc.semaphore(n))
        wt = sb("wt", [ROWS, PATCH, P])
        xt = sb("xt", [ROWS, 2, NB0 * NP_ * IMG])
        tok = sb("tok", [P, 2, NB0 * NPATCH])
        ps = [ctx.enter_context(nc.psum_tensor(f"tok_ps{i}", [P, 512], F32)) for i in range(2)]
        w_in, tok_ready, tok_copied = sem("w_in"), sem("tok_ready"), sem("tok_copied")
        x_in = [sem(f"x_in{i}") for i in range(2)]
        tok_out = [sem(f"tok_out{i}") for i in range(2)]
        block = ctx.enter_context(nc.Block())
        n = NB0 * NPATCH

        def load(sp, i, slot):
            for b in range(NB0):
                for c in range(C_IN):
                    src = x[bass.ds(i * NB0 + b, 1), c, :, :].rearrange("b (y r) w -> r (b y) w", r=PATCH)
                    dst = xt[c * PATCH:(c + 1) * PATCH, slot, b * NP_ * IMG:(b + 1) * NP_ * IMG]
                    sp.dma_start(dst.rearrange("r (y w) -> r y w", w=IMG), src).then_inc(x_in[slot], 16)

        @block.sync
        def _(sp):
            load(sp, 0, 0)
            sp.dma_start(wt[:, :, :], w_tok).then_inc(w_in, 16)
            load(sp, 1, 1)
            with sp.Fori(0, NT0 // 2 - 1) as k:
                for slot in range(2):
                    sp.wait_ge(tok_ready, k * 2 + slot + 1)
                    load(sp, k * 2 + 2 + slot, slot)

        @block.tensor
        def _(pe):
            pe.wait_ge(w_in, 16)
            with pe.Fori(0, NT0 // 2) as k:
                for slot in range(2):
                    pe.wait_ge(x_in[slot], (k + 1) * (16 * C_IN * NB0))
                    pe.wait_ge(tok_copied, k * 2 + slot + 1)
                    pix = xt[:, slot, :].rearrange("p (n s) -> p n s", s=PATCH)
                    for s in range(PATCH):
                        mm = nc.tensor.matmul(ps[slot][:, 0:n], wt[:, s, :], pix[:, :, s],
                                              start=(s == 0), stop=(s == PATCH - 1))
                    mm.then_inc(tok_ready, 1)

        @block.vector
        def _(dve):
            dve.sem_inc(tok_copied, 2)
            for slot in range(2):
                dve.sem_inc(tok_out[slot], 16)
            with dve.Fori(0, NT0 // 2) as k:
                for slot in range(2):
                    dve.wait_ge(tok_ready, k * 2 + slot + 1)
                    dve.wait_ge(tok_out[slot], k * 16 + 16)
                    nc.vector.tensor_copy(tok[:, slot, :], ps[slot][:, 0:n]).then_inc(tok_copied, 1)

        @block.scalar
        def _(act):
            with act.Fori(0, NT0 // 2) as k:
                for slot in range(2):
                    act.wait_ge(tok_copied, k * 2 + slot + 3)
                    dst = tok_scratch[:, bass.ds(k * 2 * NB0 + slot * NB0, NB0), :]
                    act.dma_start(dst, tok[:, slot, :].rearrange("p (b n) -> p b n", b=NB0)).then_inc(tok_out[slot], 16)
            for slot in range(2):
                act.wait_ge(tok_out[slot], NT0 // 2 * 16 + 16)


def fused_block(nc, txt, b_tok, cls, pos, wq, wk, wv, gn_in, rel_rev, rel_v, gn_out, wg, w1, b1, w2, b2,
                consts, tok_scratch, out):
    with ExitStack() as ctx:
        sb = lambda n, s, d=F32: ctx.enter_context(nc.sbuf_tensor(n, s, d))
        sem = lambda n: ctx.enter_context(nc.semaphore(n))

        con = sb("con", [P, NCONST])
        K = {n: con[:, a:a + w] for n, (a, w) in CO.items()}
        ident, ones, g8, g4 = K["ident"], K["ones"], K["g8"], K["g4"]
        ident_r = sb("ident_r", [32, 32], F32R)
        sel_z = sb("sel_z", [P, 64 + BH * P], F32R)
        wq_z = sb("wq_z", [P, 192])
        wk_z = sb("wk_z", [P, 192])
        wv_s = sb("wv_s", [P, P])
        vec = sb("vec", [P, 16])
        pos_s = sb("pos_s", [P, 1 + NPATCH])
        wg_s = sb("wg_s", [P, E])
        b1_s = sb("b1_s", [P, NF])
        b2_s = sb("b2_s", [P, E])
        b2x2 = sb("b2x2", [P, 1])
        half = sb("half", [P, 2])
        rw_hi = sb("rw_hi", [P, 2 * L], F32R)
        rw_lo = sb("rw_lo", [P, 2 * L], F32R)
        rv = sb("rv", [P, (LP + P) * HD])
        w1_hi = sb("w1_hi", [P, NF * P], F32R)
        w1_lo = sb("w1_lo", [P, NF * P], F32R)
        w2_s = sb("w2_s", [P, NF, P])

        tok = sb("tok2", [P, 2, NPATCH])
        txt_s = sb("txt_s", [P, 2, P])
        h = sb("h", [P, 2, L])
        h2 = sb("h2", [P, T2])
        t1 = sb("t1", [P, 2 * LP])
        t2 = sb("t2", [P, 2 * LP])
        t3 = sb("t3", [P, 2 * LP])
        q_hi, q_lo, k_hi, k_lo = (sb(n, [P, LP], F32R) for n in ("q_hi", "q_lo", "k_hi", "k_lo"))
        st = sb("st", [P, 4, 6])
        mv = sb("mv", [P, 4, 2])
        gst = sb("gst", [P, 7, 4])
        q_bd = [sb(f"q_bd_{n}", [P, OCT, BH, 8], F32R) for n in ("hi", "lo")]
        a_bd = [sb(f"a_bd_{n}", [P, OCT, BH, 8], F32R) for n in ("hi", "lo")]
        mx = sb("mx", [P, 32])
        mt = sb("mt", [32, P], F32R)
        pr = [sb(f"probs{c}", [P, OCT, BH, 8]) for c in range(2)]
        v_pad = sb("v_pad", [P, 2, H, P])
        top8 = sb("top8", [P, 4, 8])
        dl = sb("dl", [P, 8])
        wait_slot = sb("wait_slot", [P, 1])
        ep = sb("ep", [P, 8])
        ep_t = sb("ep_t", [8, P])
        x_hi = sb("x_hi", [P, T2], F32R)
        x_lo = sb("x_lo", [P, T2], F32R)
        ratio = sb("ratio", [P, T2])
        hres = sb("hres", [P, T2])
        gelu1 = sb("gelu1", [P, RING, T2])
        gelu2 = sb("gelu2", [P, RING, T2])
        o_s = sb("o_s", [P, 4, P])
        w1_st = pr[0][:, :, :, :].rearrange("p a b c -> p (a b c)")[:, 0:2048]

        bank = [ctx.enter_context(nc.psum_tensor(f"bank{i}", [P, 512], F32)) for i in range(8)]
        zb, yb, lg, pv, misc = bank[0:2], bank[2], bank[3:5], bank[5:7], bank[7]

        names = """const_in w1_in w1_split setup_dve setup_pool setup_act tok_in txt_t h_ready qk_ready v_ready
            bn mv_ready gmean gspread gvar gve grstd affine_part affine norm lo q_spread sel_done max_done mx_t mt_ready
            vt v_copied exp_done wm_done pv_done pv_ready rec_done o_part obn omv omean ospread ovar ove orstd oaff_part oaffine
            onorm h2_ready logits top_done dl_ready e_ready e1_ready p1_ready ep_tr ep_copied bcast_ready
            xp_done ffn_in xh_done gtmp sel_ready max_ready scores rel_ready z_ready z2_done g_done hs_done w2_done ot_ready o_t os_ready out_done""".split()
        S = {n: sem(n) for n in names}
        for k in ("1", "2"):
            for n in ("mean", "delta", "square", "var", "vareps", "rstd", "x"):
                S[n + k] = sem(n + k)

        GS, GB, OS, OB, BT, CL = vec[:, 0:4], vec[:, 4:8], vec[:, 8:9], vec[:, 9:10], vec[:, 10:11], vec[:, 11:12]
        V2 = lambda t: t[:, 0:T2]
        block = ctx.enter_context(nc.Block())

        def turns(eng, attend, mlp, finish):
            for s in attention_steps():
                attend(s, 0)
            finish(None, 0)
            with eng.Fori(0, PAIRS - 1) as n:
                f = 0
                for s in SCHEDULE:
                    if s == "c":
                        mlp(f, n)
                        f += 1
                    else:
                        attend(s, n + 1)
                while f < NF:
                    mlp(f, n)
                    f += 1
                finish(n, n + 1)
            for f in range(NF):
                mlp(f, PAIRS - 1)
            finish(PAIRS - 1, None)

        @block.sync
        def _(sp):
            loads = [(con[:, :], consts), (wq_z[:, 64:128], wq), (wk_z[:, 64:128], wk), (wv_s[:, :], wv),
                     (GS, gn_in[:, 0:4]), (GB, gn_in[:, 4:8]), (vec[:, 8:10], gn_out), (BT, b_tok), (CL, cls),
                     (pos_s[:, :], pos), (wg_s[:, :], wg), (b1_s[:, :], b1), (b2_s[:, :], b2),
                     (w2_s[:, :, :], w2), (rv[:, :], rel_v)]
            for dst, src in loads:
                sp.dma_start(dst, src).then_inc(S["const_in"], 16)
            for r in range(8):
                a = 126 - r
                sp.dma_start(t1[r:P - 7 + r:8, 0:2 * L - 1], rel_rev[:, a:a + 2 * L - 1]).then_inc(S["const_in"], 16)
            for piece in range(2):
                if piece:
                    sp.wait_ge(S["w1_split"], 2)
                sp.dma_start(w1_st.rearrange("d (e f) -> d e f", f=FF),
                             w1[4 * piece:4 * piece + 4, :, :].rearrange("e d f -> d e f")).then_inc(S["w1_in"], 16)

            def tokens(t):
                sp.dma_start(tok[:, :, :], tok_scratch[:, bass.ds(t * 2, 2), :]).then_inc(S["tok_in"], 16)
                sp.dma_start(txt_s[:, :, :], txt[bass.ds(t * 2, 2), :, :].rearrange("b t c -> t b c")).then_inc(S["tok_in"], 16)

            def store(n):
                sp.wait_ge(S["os_ready"], n * 2 + 4)
                for k, (a, w) in enumerate(GT):
                    sp.dma_start(out[bass.ds(n * T2 + a, w), :], o_s[0:w, k, :]).then_inc(S["out_done"], 16)

            tokens(0)
            sp.wait_ge(S["h_ready"], 2)
            tokens(1)
            with sp.Fori(0, PAIRS - 2) as n:
                sp.wait_ge(S["h_ready"], n * 2 + 4)
                tokens(n + 2)
                store(n)
            store(PAIRS - 2)
            store(PAIRS - 1)
            sp.wait_ge(S["out_done"], 64 * PAIRS + 64)

        N_CONST = 16 * (15 + 8)

        @block.tensor
        def _(pe):
            mm = nc.tensor.matmul

            def w2_step(f, n):
                pe.wait_ge(S["hs_done"], n * NF + f + 1)
                mm(yb[:, 0:T2], w2_s[:, f, :], gelu1[:, f % RING, :], start=(f == 0), stop=(f == NF - 1)).then_inc(S["w2_done"], 1)

            def mlp(f, n):
                if f == 0:
                    pe.wait_ge(S["ffn_in"], n * 4 + 4)
                if f >= 2:
                    pe.wait_ge(S["g_done"], n * (2 * NF) + 2 * (f - 2) + 1)
                z = zb[f % 2][:, 0:T2]
                w = slice(f * P, (f + 1) * P)
                mm(z, w1_hi[:, w], x_hi[:, :], start=True, stop=False)
                mm(z, w1_lo[:, w], x_hi[:, :], start=False, stop=False)
                mm(z, w1_hi[:, w], x_lo[:, :], start=False, stop=True).then_inc(S["z_ready"], 1)
                if f >= LAG:
                    w2_step(f - LAG, n)

            def finish(n, t):
                if n is not None:
                    for f in range(NF - LAG, NF):
                        w2_step(f, n)
                    pe.wait_ge(S["ot_ready"], n + 1)
                    for k, (a, w) in enumerate(GT):
                        i = nc.tensor.transpose(pv[1][0:w, k * P:(k + 1) * P], t1[:, a:a + w], ident)
                    i.then_inc(S["o_t"], 1)

            def mean_of(k, t):
                pe.wait_ge(S["h_ready" if k == "1" else "h2_ready"], t * 2 + 2)
                src = h[:, :, :].rearrange("p b l -> p (b l)") if k == "1" else h2[:, :]
                mm(misc[:, 0:T2], ones, src, start=True, stop=True).then_inc(S["mean" + k], 1)

            def var_of(k, t):
                pe.wait_ge(S["square" + k], t + 1)
                mm(misc[:, 0:T2], ones, V2(t2), start=True, stop=True).then_inc(S["var" + k], 1)

            def transpose_v(b, t):
                if b == 0:
                    pe.wait_ge(S["norm"], t * 6 + 6)
                for c, (j0, jn) in enumerate(JC):
                    i = nc.tensor.transpose(misc[0:jn, c * P:(c + 1) * P], t2[:, b * L + j0:b * L + j0 + jn], ident)
                i.then_inc(S["vt"], 1)

            def attend(s, t):
                if s == "txt":
                    pe.wait_ge(S["tok_in"], t * 32 + 32)
                    if not isinstance(t, int):
                        pe.wait_ge(S["ffn_in"], t * 4)
                    for b in range(2):
                        i = nc.tensor.transpose(misc[:, b * P:(b + 1) * P], txt_s[:, b, :], ident)
                    i.then_inc(S["txt_t"], 1)
                elif s in ("mean1", "mean2"):
                    mean_of(s[4], t)
                elif s in ("var1", "var2"):
                    var_of(s[3], t)
                elif s == "proj":
                    pe.wait_ge(S["x1"], t + 1)
                    for wz, c0 in ((wq_z, 0), (wk_z, 256)):
                        for b in range(2):
                            i = mm(misc[:, c0:c0 + L], wz[:, 64 - 64 * b:192 - 64 * b], t3[:, b * L:(b + 1) * L],
                                   start=(b == 0), stop=(b == 1))
                    i.then_inc(S["qk_ready"], 1)
                    mm(lg[0][:, 0:T2], wv_s[:, :], V2(t3), start=True, stop=True).then_inc(S["v_ready"], 1)
                elif s == "gmean":
                    pe.wait_ge(S["mv_ready"], t * 4 + 4)
                    mm(lg[1][:, 0:4], g8, mv[:, :, 0], start=True, stop=True).then_inc(S["gmean"], 1)
                elif s == "gvar":
                    pe.wait_ge(S["gspread"], t + 1)
                    mm(lg[1][:, 0:4], g8, gst[:, 3, :], start=True, stop=True).then_inc(S["gvar"], 1)
                elif s[:3] == "sel":
                    part = int(s[3])
                    k_x, q_x = (k_hi, q_hi) if part < 2 else (k_lo, q_lo)
                    if part == 0:
                        pe.wait_ge(S["norm"], t * 6 + 6)
                    if part == 2:
                        pe.wait_ge(S["lo"], t * 2 + 2)
                    for i in range(4 * part, 4 * part + 4):
                        if i >= 2:
                            pe.wait_ge(S["sel_done"], t * 16 + i - 1)
                        for k in range(2):
                            bh = 2 * (i % 8) + k
                            dst = lg[i % 2][:, k * 256:k * 256 + LP]
                            for z, x in ((0, k_x), (1, q_x)):
                                c0 = 64 - 64 * z + P * bh
                                m = mm(dst, sel_z[:, c0:c0 + P], x[:, :], start=(z == 0), stop=(z == 1))
                        m.then_inc(S["sel_ready"], 1)
                elif s == "vt0":
                    transpose_v(0, t)
                elif s[:3] == "max":
                    if s == "max0":
                        pe.wait_ge(S["q_spread"], t * 2 + 1)
                    for i in range(7) if s == "max0" else range(7, 13):
                        pe.wait_ge(S["sel_done"], t * 16 + 15 + i) if i < 2 else pe.wait_ge(S["max_done"], t * 13 + i - 1)
                        for k in range(2 if 2 * i + 1 < OCT else 1):
                            o = 2 * i + k
                            dst = lg[i % 2][:, k * 256:k * 256 + L + 1]
                            mm(dst, q_bd[0][:, o, :, :], k_hi[:, 0:L + 1], start=True, stop=False)
                            m = mm(dst, a_bd[0][:, o, :, :], rw_hi[:, 192 - 8 * o:192 - 8 * o + L + 1], start=False, stop=True)
                        m.then_inc(S["max_ready"], 1)
                elif s == "mrow":
                    pe.wait_ge(S["max_done"], t * 13 + 13)
                    pe.wait_ge(S["v_copied"], t * 4 + 2)
                    nc.tensor.transpose(misc[0:OCT, 0:P], mx[:, 0:OCT], ident).then_inc(S["mx_t"], 1)
                elif s == "vt1":
                    pe.wait_ge(S["mt_ready"], t + 1)
                    transpose_v(1, t)
                elif s == "scores":
                    pe.wait_ge(S["q_spread"], t * 2 + 2)
                    i = 0
                    for g in range(NG):
                        octs = range(g * GRP, min(OCT, (g + 1) * GRP))
                        for c, (j0, jn) in enumerate(JC):
                            pe.wait_ge(S["max_done"], t * 13 + 12 + i) if i < 2 else pe.wait_ge(S["exp_done"], t * 14 + i - 1)
                            ps = lg[(1 + i) % 2]
                            whole = ps[0:jn, 0:len(octs) * P]
                            js = slice(j0, j0 + jn)
                            os_ = slice(octs[0], octs[-1] + 1)
                            mm(whole, k_hi[:, js], q_bd[0][:, os_, :, :], start=True, stop=False)
                            mm(whole, k_lo[:, js], q_bd[0][:, os_, :, :], start=False, stop=False)
                            mm(whole, k_hi[:, js], q_bd[1][:, os_, :, :], start=False, stop=False)
                            for o in octs:
                                part = ps[0:jn, (o - octs[0]) * P:(o - octs[0] + 1) * P]
                                win = slice(192 - 8 * o + j0, 192 - 8 * o + j0 + jn)
                                mm(part, rw_hi[:, win], a_bd[0][:, o, :, :], start=False, stop=False)
                                mm(part, rw_lo[:, win], a_bd[0][:, o, :, :], start=False, stop=False)
                                mm(part, rw_hi[:, win], a_bd[1][:, o, :, :], start=False, stop=False)
                                m = mm(part, ident_r[0:OCT, o:o + 1].broadcast_to([OCT, jn]), mt[0:OCT, :],
                                       start=False, stop=(o == octs[-1]))
                            m.then_inc(S["scores"], 1)
                            i += 1
                elif s in ("pv0", "pv1"):
                    b = int(s[2])
                    pe.wait_ge(S["exp_done"], t * 14 + 14)
                    pe.wait_ge(S["v_copied"], t * 4 + 2 + 2 * b)
                    if b == 1 and not isinstance(t, int):
                        pe.wait_ge(S["os_ready"], t * 2)
                    for hh in range(H):
                        for c, (j0, jn) in enumerate(JC):
                            m = mm(pv[b][:, hh // 4 * 256:hh // 4 * 256 + LP], v_pad[0:jn, c, hh, :],
                                   pr[c][0:jn, :, H * b + hh, :], start=(hh == 0 and c == 0), stop=False,
                                   skip_group_check=True)
                    m.then_inc(S["pv_done"], 1)
                elif s == "rel":
                    for g in range(NG):
                        octs = range(g * GRP, min(OCT, (g + 1) * GRP))
                        if g >= 2:
                            pe.wait_ge(S["wm_done"], t * NG + g - 1)
                        ps = lg[(1 + g) % 2]
                        for o in octs:
                            part = ps[:, (o - octs[0]) * P:(o - octs[0] + 1) * P]
                            mm(part, rv[:, (8 * o + P) * HD:(8 * o + P) * HD + P], pr[0][:, o, :, :], start=True, stop=False)
                            m = mm(part, rv[0:JC[1][1], 8 * o * HD:8 * o * HD + P], pr[1][0:JC[1][1], o, :, :],
                                   start=False, stop=True)
                        m.then_inc(S["rel_ready"], 1)
                elif s == "place":
                    pe.wait_ge(S["wm_done"], t * NG + NG)
                    for b in range(2):
                        for hh in range(H):
                            m = mm(pv[b][:, hh // 4 * 256:hh // 4 * 256 + LP], K["place"][:, 112 - 16 * hh:112 - 16 * hh + P],
                                   pr[0][:, :, H * b + hh, :], start=False, stop=(hh == H - 1), skip_group_check=True)
                        m.then_inc(S["pv_ready"], 1)
                elif s == "omean":
                    pe.wait_ge(S["omv"], t * 2 + 2)
                    mm(misc[:, 0:2], g4, mv[:, 0:2, 0], start=True, stop=True).then_inc(S["omean"], 1)
                elif s == "ovar":
                    pe.wait_ge(S["ospread"], t + 1)
                    mm(misc[:, 0:2], g4, gst[:, 3, 0:2], start=True, stop=True).then_inc(S["ovar"], 1)
                elif s == "gate":
                    pe.wait_ge(S["x2"], t + 1)
                    for k, (a, w) in enumerate(GT):
                        m = mm(misc[0:w, 8 * k:8 * k + 8], t3[:, a:a + w], wg_s[:, :], start=True, stop=True)
                    m.then_inc(S["logits"], 1)
                elif s == "top":
                    pe.wait_ge(S["p1_ready"], t + 1)
                    nc.tensor.transpose(misc[0:8, 0:GT[0][1]], ep[0:GT[0][1], :], ident[0:GT[0][1], 0:GT[0][1]]).then_inc(S["ep_tr"], 1)
                elif s == "bcast":
                    pe.wait_ge(S["ep_copied"], t + 1)
                    for q, ps in ((0, misc), (4, pv[0])):
                        for k, (a, w) in enumerate(GT):
                            m = mm(ps[:, a:a + w], ident[0:8, q + k:q + k + 1].broadcast_to([8, P]), ep_t[:, 0:w],
                                   start=True, stop=True)
                    m.then_inc(S["bcast_ready"], 1)

            pe.wait_ge(S["const_in"], N_CONST)
            pe.wait_ge(S["setup_dve"], 16)
            pe.wait_ge(S["w1_split"], 4)
            turns(pe, attend, mlp, finish)

        @block.vector
        def _(dve):
            v = nc.vector

            def carry_wait():
                v.memset(wait_slot[:, :], 0.0)

            def mlp(f, n):
                dve.wait_ge(S["z_ready"], n * NF + f + 1)
                if f >= RING:
                    dve.wait_ge(S["hs_done"], n * NF + f - RING + 1)
                v.tensor_tensor(gelu2[:, f % RING, :], zb[f % 2][:, 0:T2], ratio[:, :], ALU.mult).then_inc(S["z2_done"], 1)

            def finish(n, t):
                if n is not None:
                    dve.wait_ge(S["w2_done"], n * NF + NF)
                    v.tensor_tensor(V2(t1), yb[:, 0:T2], hres[:, :], ALU.add).then_inc(S["ot_ready"], 1)
                if t is not None:
                    dve.wait_ge(S["xp_done"], t + 1)
                    v.tensor_copy(x_hi[:, :], V2(t2)).then_inc(S["xh_done"], 1)
                    v.tensor_copy(ratio[:, :], misc[:, 0:T2]).then_inc(S["ffn_in"], 1)
                    if n is not None:
                        dve.wait_ge(S["ot_ready"], n + 1)
                    v.tensor_scalar(hres[:, :], h2[:, :], b2x2[:, :], None, ALU.add).then_inc(S["ffn_in"], 1)
                    dve.wait_ge(S["xh_done"], t + 1)
                    v.tensor_tensor(x_lo[:, :], V2(t2), x_hi[:, :].bitcast(F32), ALU.subtract).then_inc(S["ffn_in"], 2)
                if n is not None:
                    dve.wait_ge(S["o_t"], n + 1)
                    dve.wait_ge(S["out_done"], n * 64 + 64)
                    v.tensor_copy(o_s[0:97, 0:2, :], pv[1][0:97, 0:2 * P].rearrange("p (k c) -> p k c", k=2)).then_inc(S["os_ready"], 1)
                    v.tensor_copy(o_s[0:96, 2:4, :], pv[1][0:96, 2 * P:4 * P].rearrange("p (k c) -> p k c", k=2)).then_inc(S["os_ready"], 1)

            def layernorm(s, k, t):
                src = h[:, :, :].rearrange("p b l -> p (b l)") if k == "1" else h2[:, :]
                if s == "mean":
                    dve.wait_ge(S["mean" + k], t + 1)
                    v.tensor_tensor(V2(t1), src, misc[:, 0:T2], ALU.subtract).then_inc(S["delta" + k], 1)
                    dve.wait_ge(S["delta" + k], t + 1)
                    v.tensor_tensor(V2(t2), V2(t1), V2(t1), ALU.mult).then_inc(S["square" + k], 1)
                else:
                    dve.wait_ge(S["var" + k], t + 1)
                    v.tensor_scalar(V2(t2), misc[:, 0:T2], LN_EPS, None, ALU.add).then_inc(S["vareps" + k], 1)
                    dve.wait_ge(S["rstd" + k], t + 1)
                    v.tensor_tensor(V2(t3), V2(t1), V2(t2), ALU.mult).then_inc(S["x" + k], 1)

            def group_spread(m, psum, ready, done, t):
                gm, dm, d2, sp_ = (gst[:, i, 0:m] for i in range(4))
                dve.wait_ge(ready, t + 1)
                v.tensor_copy(gm, psum)
                v.tensor_tensor(dm, mv[:, 0:m, 0], psum, ALU.subtract).then_inc(S["gtmp"], 1)
                dve.wait_ge(S["gtmp"], self_count(t, m, 1))
                v.tensor_tensor(d2, dm, dm, ALU.mult).then_inc(S["gtmp"], 1)
                dve.wait_ge(S["gtmp"], self_count(t, m, 2))
                v.tensor_tensor(sp_, d2, mv[:, 0:m, 1], ALU.add).then_inc(done, 1)

            def self_count(t, m, k):
                return t * 4 + (0 if m == 4 else 2) + k

            def group_affine(m, psum, ready, ve, rstd, part, done, scale, bias, t):
                gm, _, d2, _, rs, sc, bi = (gst[:, i, 0:m] for i in range(7))
                dve.wait_ge(ready, t + 1)
                v.tensor_scalar(rs, psum, GN_EPS, None, ALU.add).then_inc(ve, 1)
                dve.wait_ge(rstd, t + 1)
                v.tensor_tensor(sc, scale, rs, ALU.mult).then_inc(part, 1)
                dve.wait_ge(part, t * 2 + 1)
                v.tensor_tensor(d2, gm, sc, ALU.mult).then_inc(part, 1)
                dve.wait_ge(part, t * 2 + 2)
                v.tensor_tensor(bi, bias, d2, ALU.subtract).then_inc(done, 1)

            def attend(s, t):
                if s == "txt":
                    dve.wait_ge(S["tok_in"], t * 32 + 32)
                    v.scalar_tensor_tensor(out=h[:, :, 1:1 + NPATCH], in0=tok[:, :, :], scalar=BT,
                                           in1=pos_s[:, 1:].unsqueeze(1).broadcast_to([P, 2, NPATCH]),
                                           op0=ALU.add, op1=ALU.mult).then_inc(S["h_ready"], 1)
                    dve.wait_ge(S["txt_t"], t + 1)
                    v.tensor_copy(h[:, :, 1 + NPATCH:], misc[:, 0:2 * P].rearrange("p (b l) -> p b l", b=2)).then_inc(S["h_ready"], 1)
                elif s in ("mean1", "mean2"):
                    layernorm("mean", s[4], t)
                elif s in ("var1", "var2"):
                    layernorm("var", s[3], t)
                    if s == "var2":
                        pass
                elif s == "proj":
                    dve.wait_ge(S["qk_ready"], t + 1)
                    v.bn_stats(st[:, 0, :], misc[:, 0:L]).then_inc(S["bn"], 1)
                    v.bn_stats(st[:, 1, :], misc[:, 256:256 + L]).then_inc(S["bn"], 1)
                    dve.wait_ge(S["v_ready"], t + 1)
                    for b in range(2):
                        v.bn_stats(st[:, 2 + b, :], lg[0][:, b * L:(b + 1) * L]).then_inc(S["bn"], 1)
                    dve.wait_ge(S["bn"], t * 4 + 4)
                    carry_wait()
                    for k in range(4):
                        v.bn_aggr(mv[:, k, :], st[:, k, :]).then_inc(S["mv_ready"], 1)
                elif s == "gmean":
                    group_spread(4, lg[1][:, 0:4], S["gmean"], S["gspread"], t)
                elif s == "gvar":
                    group_affine(4, lg[1][:, 0:4], S["gvar"], S["gve"], S["grstd"], S["affine_part"], S["affine"], GS, GB, t)
                    dve.wait_ge(S["norm"], t * 6 + 4)
                    for x, lo, hi in ((t1[:, 0:L], q_lo, q_hi), (t1[:, LP:LP + L], k_lo, k_hi)):
                        v.tensor_tensor(lo[:, 0:L], x, hi[:, 0:L].bitcast(F32), ALU.subtract).then_inc(S["lo"], 1)
                elif s[:3] == "sel":
                    part = int(s[3])
                    for i in range(4 * part, 4 * part + 4):
                        bh = 2 * (i % 8)
                        dve.wait_ge(S["sel_ready"], t * 16 + i + 1)
                        v.tensor_tensor(a_bd[i // 8][:, :, bh:bh + 2, :].rearrange("p o b r -> p b o r"),
                                        lg[i % 2][:, :].rearrange("p (b x) -> p b x", b=2)[:, :, 0:LP].rearrange("p b (o r) -> p b o r", r=8),
                                        K["mask_q"].unsqueeze(1).unsqueeze(1).broadcast_to([P, 2, OCT, 8]),
                                        ALU.mult).then_inc(S["sel_done"], 1)
                elif s[:3] == "max":
                    for i in range(7) if s == "max0" else range(7, 13):
                        dve.wait_ge(S["max_ready"], t * 13 + i + 1)
                        w = 2 if 2 * i + 1 < OCT else 1
                        v.tensor_reduce(mx[:, 2 * i:2 * i + w], lg[i % 2][:, :].rearrange("p (k x) -> p k x", k=2)[:, 0:w, 0:L],
                                        AX, ALU.max).then_inc(S["max_done"], 1)
                elif s == "mrow":
                    dve.wait_ge(S["mx_t"], t + 1)
                    v.tensor_scalar(mt[0:OCT, :], misc[0:OCT, 0:P], -1.0, None, ALU.mult).then_inc(S["mt_ready"], 1)
                elif s == "rel":
                    for g in range(NG):
                        w = min(OCT, (g + 1) * GRP) - g * GRP
                        dve.wait_ge(S["rel_ready"], t * NG + g + 1)
                        v.tensor_tensor(pr[0][:, g * GRP:g * GRP + w, :, :].rearrange("p o b r -> p (o b) r"),
                                        lg[(1 + g) % 2][:, 0:w * P].rearrange("p (x r) -> p x r", r=8),
                                        K["mask_r"].unsqueeze(1).broadcast_to([P, w * BH, 8]), ALU.mult).then_inc(S["wm_done"], 1)
                elif s == "place":
                    dve.wait_ge(S["pv_ready"], t * 2 + 2)
                    for b in range(2):
                        for a, n_, d_ in ((0, 0, 64), (256, 64, 0)):
                            v.reciprocal(t3[n_:n_ + 64, b * L:(b + 1) * L], pv[b][d_:d_ + 64, a:a + L]).then_inc(S["rec_done"], 1)
                    k = 0
                    for b in range(2):
                        for a, n_ in ((0, 0), (256, 64)):
                            k += 1
                            dve.wait_ge(S["rec_done"], t * 4 + k)
                            v.tensor_tensor(t1[n_:n_ + 64, b * L:(b + 1) * L], pv[b][n_:n_ + 64, a:a + L],
                                            t3[n_:n_ + 64, b * L:(b + 1) * L], ALU.mult).then_inc(S["o_part"], 1)
                    for b in range(2):
                        dve.wait_ge(S["o_part"], t * 4 + 2 * b + 2)
                        v.bn_stats(st[:, b, :], t1[:, b * L:(b + 1) * L]).then_inc(S["obn"], 1)
                    dve.wait_ge(S["obn"], t * 2 + 2)
                    carry_wait()
                    for b in range(2):
                        v.bn_aggr(mv[:, b, :], st[:, b, :]).then_inc(S["omv"], 1)
                elif s == "omean":
                    group_spread(2, misc[:, 0:2], S["omean"], S["ospread"], t)
                elif s == "ovar":
                    group_affine(2, misc[:, 0:2], S["ovar"], S["ove"], S["orstd"], S["oaff_part"], S["oaffine"],
                                 OS.broadcast_to([P, 2]), OB.broadcast_to([P, 2]), t)
                    for b in range(2):
                        dve.wait_ge(S["onorm"], t * 2 + b + 1)
                        bs = slice(b * L, (b + 1) * L)
                        v.tensor_tensor(h2[:, bs], h[:, b, :], t2[:, bs], ALU.add).then_inc(S["h2_ready"], 1)
                elif s == "gate":
                    dve.wait_ge(S["logits"], t + 1)
                    carry_wait()
                    for k, (a, w) in enumerate(GT):
                        v.max(top8[0:w, k, :], misc[0:w, 8 * k:8 * k + 8]).then_inc(S["top_done"], 1)
                    dve.wait_ge(S["top_done"], t * 4 + 4)
                    v.tensor_tensor(dl[0:97, 0:4], top8[0:97, :, 1], top8[0:97, :, 0], ALU.subtract).then_inc(S["dl_ready"], 1)
                    dve.wait_ge(S["e_ready"], t + 1)
                    v.tensor_scalar(dl[0:97, 4:8], ep[0:97, 0:4], 1.0, None, ALU.add).then_inc(S["e1_ready"], 1)
                    dve.wait_ge(S["e1_ready"], t + 1)
                    v.reciprocal(ep[0:97, 4:8], dl[0:97, 4:8]).then_inc(S["p1_ready"], 1)
                elif s == "top":
                    dve.wait_ge(S["ep_tr"], t + 1)
                    v.tensor_copy(ep_t[:, 0:97], misc[0:8, 0:97]).then_inc(S["ep_copied"], 1)
                elif s == "bcast":
                    dve.wait_ge(S["bcast_ready"], t + 1)
                    v.tensor_tensor(V2(t2), V2(t3), pv[0][:, 0:T2], ALU.mult).then_inc(S["xp_done"], 1)

            z = S["setup_dve"]
            v.memset(wq_z[:, 0:64], 0.0); v.memset(wq_z[:, 128:192], 0.0)
            v.memset(wk_z[:, 0:64], 0.0); v.memset(wk_z[:, 128:192], 0.0)
            for x in (q_hi, q_lo, k_hi, k_lo):
                v.memset(x[:, :].bitcast(F32), 0.0).then_inc(z, 1)
            v.memset(half[:, 0:1], -0.5).then_inc(z, 1)
            v.memset(half[:, 1:2], 2.718281828459045).then_inc(z, 1)
            v.memset(top8[:, :, :], 0.0).then_inc(z, 1)
            v.memset(v_pad[:, :, :, :], 0.0).then_inc(z, 1)
            v.memset(sel_z[:, :].bitcast(F32), 0.0).then_inc(z, 1)
            dve.wait_ge(z, 9)
            for hh in range(H):
                c0 = (64 if hh < 4 else 0) + (hh % 4) * HD
                last = v.memset(v_pad[:, :, hh, c0:c0 + HD], 1.0)
            last.then_inc(z, 1)
            dve.wait_ge(S["const_in"], N_CONST)
            v.memset(t1[:, 2 * L - 1:2 * L], 0.0).then_inc(z, 1)
            v.tensor_copy(ident_r[:, :], con[0:32, 0:32])
            v.tensor_tensor(sel_z[:, 64:].rearrange("p (b z e r) -> p b z e r", b=BH, z=2, e=8)[:, :, 0, :, :],
                            K["mask_bh"].unsqueeze(2).unsqueeze(3).broadcast_to([P, BH, 8, 8]),
                            K["mask_q"].unsqueeze(1).unsqueeze(3).broadcast_to([P, BH, 8, 8]), ALU.mult)
            for b in range(2):
                v.tensor_tensor(h[:, b, 0:1], CL, pos_s[:, 0:1], ALU.mult)
            v.tensor_reduce(b2x2[:, :], b2_s[:, :], AX, ALU.add).then_inc(z, 1)
            dve.wait_ge(z, 12)
            v.tensor_scalar(b2x2[:, :], b2x2[:, :], 2.0, None, ALU.mult).then_inc(z, 1)
            v.tensor_copy(rw_hi[:, :], V2(t1)).then_inc(z, 1)
            dve.wait_ge(z, 14)
            v.tensor_tensor(rw_lo[:, :], V2(t1), rw_hi[:, :].bitcast(F32), ALU.subtract).then_inc(z, 2)
            for piece in range(2):
                dve.wait_ge(S["w1_in"], 16 * piece + 16)
                a = slice(2048 * piece, 2048 * piece + 2048)
                v.tensor_copy(w1_hi[:, a], w1_st).then_inc(S["w1_split"], 1)
                dve.wait_ge(S["w1_split"], 2 * piece + 1)
                v.tensor_tensor(w1_lo[:, a], w1_st, w1_hi[:, a].bitcast(F32), ALU.subtract).then_inc(S["w1_split"], 1)
            dve.sem_inc(S["out_done"], 64)
            dve.sem_inc(S["os_ready"], 2)
            turns(dve, attend, mlp, finish)

        @block.scalar
        def _(act):
            a = nc.scalar.activation

            def mlp(f, n):
                act.wait_ge(S["z2_done"], n * NF + f + 1)
                if f >= RING:
                    act.wait_ge(S["w2_done"], n * NF + f - RING + 1)
                a(gelu1[:, f % RING, :], zb[f % 2][:, 0:T2], ACT.Gelu, bias=b1_s[:, f:f + 1]).then_inc(S["g_done"], 1)
                a(gelu2[:, f % RING, :], gelu2[:, f % RING, :], ACT.Gelu, bias=b1_s[:, f:f + 1]).then_inc(S["g_done"], 1)

            def copy_v(b, t):
                act.wait_ge(S["vt"], t * 2 + b + 1)
                if b == 1:
                    act.wait_ge(S["pv_done"], t * 2 + 1)
                for c, (j0, jn) in enumerate(JC):
                    blk = v_pad[0:jn, c, :, :].rearrange("p h n -> p (h n)")
                    dst = bass.AP(tensor=blk.tensor, offset=blk.offset, ap=[list(blk.ap[0]), [P + HD, H], [1, HD]])
                    a(dst, misc[0:jn, c * P:(c + 1) * P].rearrange("p (h d) -> p h d", h=H), ACT.Copy).then_inc(S["v_copied"], 1)

            def attend(s, t):
                if s == "gvar":
                    act.wait_ge(S["affine"], t + 1)
                    sc, bi = gst[:, 5, :], gst[:, 6, :]
                    for k, ps, hi, val in ((0, misc[:, 0:L], q_hi[:, 0:L], t1[:, 0:L]),
                                           (1, misc[:, 256:256 + L], k_hi[:, 0:L], t1[:, LP:LP + L])):
                        for dst in (hi, val):
                            a(dst, ps, ACT.Identity, bias=bi[:, k:k + 1], scale=sc[:, k:k + 1]).then_inc(S["norm"], 1)
                    for b in range(2):
                        a(t2[:, b * L:(b + 1) * L], lg[0][:, b * L:(b + 1) * L], ACT.Identity,
                          bias=bi[:, 2 + b:3 + b], scale=sc[:, 2 + b:3 + b]).then_inc(S["norm"], 1)
                elif s == "vt0":
                    copy_v(0, t)
                elif s == "scores":
                    i = 0
                    for g in range(NG):
                        w = min(OCT, (g + 1) * GRP) - g * GRP
                        for c, (j0, jn) in enumerate(JC):
                            act.wait_ge(S["scores"], t * 14 + i + 1)
                            a(pr[c][0:jn, g * GRP:g * GRP + w, :, :].rearrange("p o b r -> p (o b r)"),
                              lg[(1 + i) % 2][0:jn, 0:w * P], ACT.Exp).then_inc(S["exp_done"], 1)
                            i += 1
                elif s == "pv0":
                    copy_v(1, t)
                elif s == "ovar":
                    act.wait_ge(S["oaffine"], t + 1)
                    for b in range(2):
                        bs = slice(b * L, (b + 1) * L)
                        a(t2[:, bs], t1[:, bs], ACT.Identity, bias=gst[:, 6, b:b + 1], scale=gst[:, 5, b:b + 1]).then_inc(S["onorm"], 1)

            act.wait_ge(S["setup_dve"], 10)
            act.wait_ge(S["const_in"], N_CONST)
            turns(act, attend, mlp, lambda n, t: None)

        @block.gpsimd
        def _(pool):
            g = nc.gpsimd

            def mlp(f, n):
                pool.wait_ge(S["g_done"], n * (2 * NF) + 2 * f + 2)
                g.tensor_tensor(gelu1[:, f % RING, :], gelu1[:, f % RING, :], gelu2[:, f % RING, :], ALU.add).then_inc(S["hs_done"], 1)

            def rsqrt(x, ready, done, t):
                pool.wait_ge(ready, t + 1)
                g.tensor_tensor(x, x, half[:, 0:1].broadcast_to(list(x.shape)), ALU.pow).then_inc(done, 1)

            def attend(s, t):
                if s in ("var1", "var2"):
                    rsqrt(V2(t2), S["vareps" + s[3]], S["rstd" + s[3]], t)
                elif s == "gvar":
                    rsqrt(gst[:, 4, :], S["gve"], S["grstd"], t)
                elif s == "ovar":
                    rsqrt(gst[:, 4, 0:2], S["ove"], S["orstd"], t)
                elif s in ("sel0", "sel1"):
                    k = int(s[3])
                    x = (q_hi, q_lo)[k]
                    if k == 0:
                        pool.wait_ge(S["norm"], t * 6 + 4)
                    else:
                        pool.wait_ge(S["lo"], t * 2 + 2)
                    g.tensor_tensor(q_bd[k][:, :, :, :],
                                    x[:, :].bitcast(F32).rearrange("p (o r) -> p o r", r=8).unsqueeze(2).broadcast_to([P, OCT, BH, 8]),
                                    K["mask_bh"].unsqueeze(1).unsqueeze(3).broadcast_to([P, OCT, BH, 8]), ALU.mult).then_inc(S["q_spread"], 1)
                elif s == "gate":
                    pool.wait_ge(S["dl_ready"], t + 1)
                    g.tensor_tensor(ep[0:97, 0:4], half[0:97, 1:2].broadcast_to([97, 4]), dl[0:97, 0:4], ALU.pow).then_inc(S["e_ready"], 1)

            pool.wait_ge(S["setup_dve"], 10)
            pool.wait_ge(S["const_in"], N_CONST)
            turns(pool, attend, mlp, lambda n, t: None)


def build(nc, a, out):
    tok_scratch = nc.dram_tensor("tok_scratch", (P, B, NPATCH), F32, kind="Internal").ap()
    patch_embed(nc, a["x"], a["w_tok"], tok_scratch)
    fused_block(nc, a["txt"], a["b_tok"], a["cls"], a["pos"], a["wq"], a["wk"], a["wv"], a["gn_in"], a["rel_rev"],
                a["rel_v"], a["gn_out"], a["wg"], a["w1"], a["b1"], a["w2"], a["b2"], a["consts"], tok_scratch,
                out.rearrange("b l c -> (b l) c"))


def shape_constants(np):
    c = np.zeros((P, NCONST), np.float32)
    p = np.arange(P)

    def put(name, value):
        a, w = CO[name]
        c[:, a:a + w] = value

    put("ident", np.eye(P))
    put("ones", 1.0 / P)
    put("g8", (p[:, None] // 8 == p[None] // 8) / 8.0)
    put("g4", (p[:, None] // 4 == p[None] // 4) / 4.0)
    put("mask_bh", p[:, None] // DK == np.arange(BH)[None])
    put("mask_r", p[:, None] // HD == np.arange(8)[None])
    put("mask_q", p[:, None] % 8 == np.arange(8)[None])
    w = np.zeros((P, 112 + HD + 112))
    w[:, 112:112 + HD] = p[:, None] % HD == np.arange(HD)[None]
    put("place", w)
    return c


def kernel(**inputs):
    import numpy as np
    import concourse.bacc as bacc
    from concourse.bass_utils import run_bass_kernel_spmd

    i = {k: np.asarray(v) for k, v in inputs.items()}
    qkv = i["L0_attn_W_qkv"].reshape(P, H, 2 * HD)
    parts = (slice(0, DK), slice(DK, 2 * DK), slice(2 * DK, 2 * HD))

    def gn_columns(v):
        q, k, val = (v.reshape(H, 2 * HD)[:, s].reshape(-1) for s in parts)
        return [np.concatenate([q, q]), np.concatenate([k, k]), val, val]

    rel = i["L0_attn_rel_emb"]
    arrays = {
        "x": i["x"], "txt": i["txt"],
        "w_tok": i["L0_tok_W"].reshape(P, ROWS, PATCH).transpose(1, 2, 0),
        "b_tok": i["L0_tok_b"].reshape(P, 1), "cls": i["L0_tok_class_token"].reshape(P, 1),
        "pos": i["L0_tok_pos_embed"].T,
        "wq": qkv[:, :, parts[0]].reshape(P, -1), "wk": qkv[:, :, parts[1]].reshape(P, -1), "wv": qkv[:, :, parts[2]].reshape(P, -1),
        "gn_in": np.stack(gn_columns(i["L0_attn_gn_qkv_scale"]) + gn_columns(i["L0_attn_gn_qkv_bias"]), 1),
        "rel_rev": rel[0:HD, ::-1], "rel_v": rel[HD:2 * HD].T[np.maximum(np.arange(LP + P)[None] - np.arange(P)[:, None] + 64, 0)].reshape(P, -1),
        "gn_out": np.stack([i["L0_attn_gn_out_scale"], i["L0_attn_gn_out_bias"]], 1),
        "wg": i["L0_ffn_Wg"], "w1": i["L0_ffn_W1"], "b1": i["L0_ffn_b1"].reshape(NF, P).T,
        "w2": i["L0_ffn_W2"].reshape(NF, P, P).transpose(1, 0, 2), "b2": i["L0_ffn_b2"].T,
        "consts": shape_constants(np),
    }
    arrays = {f"in_{k}": np.ascontiguousarray(v) for k, v in arrays.items()}
    nc = bacc.Bacc("TRN2", target_bir_lowering=False, num_devices=1)
    aps = {k[3:]: nc.dram_tensor(k, v.shape, mybir.dt.from_np(v.dtype), kind="ExternalInput").ap() for k, v in arrays.items()}
    out = nc.dram_tensor("out", (B, L, P), F32, kind="ExternalOutput").ap()
    build(nc, aps, out)
    return run_bass_kernel_spmd(nc, [arrays], core_ids=[0]).results[0]["out"]
```

```python
from contextlib import ExitStack

import concourse.bass as bass
from concourse import mybir

F32 = mybir.dt.float32
F32R = mybir.dt.float32r
BF16 = mybir.dt.bfloat16
ACT = mybir.ActivationFunctionType
ALU = mybir.AluOpType
AX = mybir.AxisListType.X

P = 128
B, C_IN, IMG = 64, 3, 224
NP_, PATCH = 8, 28
NPATCH = NP_ * NP_
ROWS = C_IN * PATCH
TXT = 128
L = 1 + NPATCH + TXT
PAIRS = B // 2
T2 = 2 * L
H, HD, DK = 8, 16, 8
BH = 2 * H
OCT = 25
LP = 8 * OCT
GRP = 4
NG = (OCT + GRP - 1) // GRP
JC = [(0, 128), (128, L - 128)]
E, FF = 8, 512
NF = E * FF // P
RING = 4
LAG = 3
GT = [(0, 97), (97, 97), (194, 96), (290, 96)]
GO = [0, 97, L, L + 96]
GW = 97
LN_EPS, GN_EPS = 1e-5, 1e-4
NB0 = 4
NT0 = B // NB0

CO = {}
_at = 0
for _n, _w in (("ident", P), ("ones", P), ("g8", P), ("g4", P), ("mask_bh", BH), ("mask_r", 8), ("mask_q", 8),
               ("place", 112 + HD + 112)):
    CO[_n] = (_at, _w)
    _at += _w
NCONST = _at

EARLY = "txt mean1 var1 inv1 bc1 proj gmean gvar gaff glo qs0 qs1 sel0 sel1 sel2".split()
OUTPUT = "w2t otr ocopy".split()
SCHEDULE = (
    "c sel3 c sel4 c qs2 sel5 c sel6 c qs3 sel7 c vt0 hkeep max0 c max1 c max2 c mrow c vt1 scores pv0 pv1 rel "
    "place0 txt c place1 mean1 c c omean var1 c ovar c inv1 oaff c bc1 oh2 c proj c mean2 gmean c c var2 gvar c "
    "inv2 gaff c bc2 c glo c gate c gate2 c c top c c bcast w2t xin w2t sel0 w2t qs0 a otr sel1 a ocopy hres qs1 sel2 a"
).split()
AHEAD = SCHEDULE.count("a")

assert SCHEDULE.count("c") + AHEAD == NF and SCHEDULE.count("w2t") == LAG and AHEAD <= LAG


MAX_FILLS = {"max0": range(4), "max1": range(4, 8), "max2": range(8, 13)}


def is_first(t):
    return isinstance(t, int) and t == 0


def patch_embed(nc, x, w_tok, tok_scratch):
    with ExitStack() as ctx:
        sb = lambda n, s, d=F32: ctx.enter_context(nc.sbuf_tensor(n, s, d))
        sem = lambda n: ctx.enter_context(nc.semaphore(n))
        wt = sb("wt", [ROWS, PATCH, P])
        xt = sb("xt", [ROWS, 2, NB0 * NP_ * IMG])
        tok = sb("tok", [P, 2, NB0 * NPATCH])
        ps = [ctx.enter_context(nc.psum_tensor(f"tok_ps{i}", [P, 512], F32)) for i in range(2)]
        w_in, tok_ready, tok_copied = sem("w_in"), sem("tok_ready"), sem("tok_copied")
        x_in = [sem(f"x_in{i}") for i in range(2)]
        tok_out = [sem(f"tok_out{i}") for i in range(2)]
        block = ctx.enter_context(nc.Block())
        n = NB0 * NPATCH

        def load(sp, i, slot):
            for b in range(NB0):
                for c in range(C_IN):
                    src = x[bass.ds(i * NB0 + b, 1), c, :, :].rearrange("b (y r) w -> r (b y) w", r=PATCH)
                    dst = xt[c * PATCH:(c + 1) * PATCH, slot, b * NP_ * IMG:(b + 1) * NP_ * IMG]
                    sp.dma_start(dst.rearrange("r (y w) -> r y w", w=IMG), src).then_inc(x_in[slot], 16)

        @block.sync
        def _(sp):
            load(sp, 0, 0)
            sp.dma_start(wt[:, :, :], w_tok).then_inc(w_in, 16)
            load(sp, 1, 1)
            with sp.Fori(0, NT0 // 2 - 1) as k:
                for slot in range(2):
                    sp.wait_ge(tok_ready, k * 2 + slot + 1)
                    load(sp, k * 2 + 2 + slot, slot)

        @block.tensor
        def _(pe):
            pe.wait_ge(w_in, 16)
            with pe.Fori(0, NT0 // 2) as k:
                for slot in range(2):
                    pe.wait_ge(x_in[slot], (k + 1) * (16 * C_IN * NB0))
                    pe.wait_ge(tok_copied, k * 2 + slot + 1)
                    pix = xt[:, slot, :].rearrange("p (n s) -> p n s", s=PATCH)
                    for s in range(PATCH):
                        mm = nc.tensor.matmul(ps[slot][:, 0:n], wt[:, s, :], pix[:, :, s],
                                              start=(s == 0), stop=(s == PATCH - 1))
                    mm.then_inc(tok_ready, 1)

        @block.vector
        def _(dve):
            dve.sem_inc(tok_copied, 2)
            for slot in range(2):
                dve.sem_inc(tok_out[slot], 16)
            with dve.Fori(0, NT0 // 2) as k:
                for slot in range(2):
                    dve.wait_ge(tok_ready, k * 2 + slot + 1)
                    dve.wait_ge(tok_out[slot], k * 16 + 16)
                    nc.vector.tensor_copy(tok[:, slot, :], ps[slot][:, 0:n]).then_inc(tok_copied, 1)

        @block.scalar
        def _(act):
            with act.Fori(0, NT0 // 2) as k:
                for slot in range(2):
                    act.wait_ge(tok_copied, k * 2 + slot + 3)
                    dst = tok_scratch[:, bass.ds(k * 2 * NB0 + slot * NB0, NB0), :]
                    act.dma_start(dst, tok[:, slot, :].rearrange("p (b n) -> p b n", b=NB0)).then_inc(tok_out[slot], 16)
            for slot in range(2):
                act.wait_ge(tok_out[slot], NT0 // 2 * 16 + 16)


def fused_block(nc, txt, b_tok, cls, pos, wq, wk, wv, gn_in, rel_rev, rel_v, gn_out, wg, w1, b1, w2, b2,
                consts, tok_scratch, out):
    with ExitStack() as ctx:
        sb = lambda n, s, d=F32: ctx.enter_context(nc.sbuf_tensor(n, s, d))
        sem = lambda n: ctx.enter_context(nc.semaphore(n))

        con = sb("con", [P, NCONST])
        K = {n: con[:, a:a + w] for n, (a, w) in CO.items()}
        ident, ones, g8, g4 = K["ident"], K["ones"], K["g8"], K["g4"]
        pick_o = sb("pick_o", [64, 32], BF16)
        sel_z = sb("sel_z", [P, 64 + BH * P], F32R)
        wq_z = sb("wq_z", [P, 192])
        wk_z = sb("wk_z", [P, 192])
        wv_s = sb("wv_s", [P, P])
        vec = sb("vec", [P, 16])
        pos_s = sb("pos_s", [P, 1 + NPATCH])
        wg_s = sb("wg_s", [P, E])
        b1_s = sb("b1_s", [P, NF])
        b2_s = sb("b2_s", [P, E])
        b2x2 = sb("b2x2", [P, 1])
        half = sb("half", [P, 2])
        rw_hi = sb("rw_hi", [P, 2 * L], F32R)
        rw_lo = sb("rw_lo", [P, 2 * L], F32R)
        rv = sb("rv", [P, (LP + P) * HD])
        w1_hi = sb("w1_hi", [P, NF * P], F32R)
        w1_lo = sb("w1_lo", [P, NF * P], F32R)
        w2_s = sb("w2_s", [P, NF, P])

        tok = sb("tok2", [P, 2, NPATCH])
        txt_s = sb("txt_s", [P, 2, P])
        h = sb("h", [P, 2, L])
        h2 = sb("h2", [P, T2])
        t1 = sb("t1", [P, 2 * LP])
        t2 = sb("t2", [P, 2 * LP])
        e1 = sb("e1", [P, 2 * LP])
        e2 = sb("e2", [P, 2 * LP])
        q_hi, q_lo, k_hi, k_lo = (sb(n, [P, LP], F32R) for n in ("q_hi", "q_lo", "k_hi", "k_lo"))
        st, st_o = sb("st", [P, 4, 6]), sb("st_o", [P, 2, 6])
        mv, mv_o = sb("mv", [P, 4, 2]), sb("mv_o", [P, 2, 2])
        gst, gst_o = (sb(n, [P, 7, 4]) for n in ("gst", "gst_o"))
        q_bd = [sb(f"q_bd_{n}", [P, OCT, BH, 8], F32R) for n in ("hi", "lo")]
        a_bd = [sb(f"a_bd_{n}", [P, OCT, BH, 8], F32R) for n in ("hi", "lo")]
        mx = sb("mx", [P, 32])
        mt = sb("mt", [64, P], BF16)
        pr = [sb(f"probs{c}", [P, OCT, BH, 8]) for c in range(2)]
        v_pad = sb("v_pad", [P, 2, H, P])
        top8 = sb("top8", [P, 4, 8])
        dl = sb("dl", [P, 8])
        wait_slot = sb("wait_slot", [P, 4])
        ep = sb("ep", [P, 8])
        ep_t = sb("ep_t", [8, GW])
        rs1, rs2 = sb("rs1", [P, 4]), sb("rs2", [P, 4])
        rs1_t, rs2_t = sb("rs1_t", [4, GW]), sb("rs2_t", [4, GW])
        x_hi = sb("x_hi", [P, T2], F32R)
        x_lo = sb("x_lo", [P, T2], F32R)
        ratio = sb("ratio", [P, T2])
        hres = sb("hres", [P, T2])
        gelu1 = sb("gelu1", [P, RING, T2])
        gelu2 = sb("gelu2", [P, RING, T2])
        o_s = sb("o_s", [P, 4, P])
        w1_st = pr[0][:, :, :, :].rearrange("p a b c -> p (a b c)")[:, 0:2048]

        bank = [ctx.enter_context(nc.psum_tensor(f"bank{i}", [P, 512], F32)) for i in range(8)]
        zb, yb, lg, pv, misc = bank[0:2], bank[2], bank[3:5], bank[5:7], bank[7]
        LN = {"1": (misc, e1, e2, rs1, rs1_t), "2": (pv[0], t1, t2, rs2, rs2_t)}

        names = """const_in w1_in w1_split setup_dve setup_pool setup_act tok_in txt_t h_ready qk_ready v_ready
            bn mv_ready gmean gspread gvar gve grstd affine_part affine norm lo q_spread sel_done max_done mx_t mt_ready
            vt v_copied exp_done wm_done pv_done pv_ready rec_done o_part obn omv omean ospread ovar ove orstd oaff_part oaffine
            onorm h2_ready logits top_done dl_ready e_ready e1_ready p1_ready ep_tr ep_copied bcast_ready
            xp_done ffn_in xh_done gtmp otmp mt_hi sel_ready max_ready scores rel_ready z_ready z2_done g_done hres_done h_kept hs_done w2_done ot_ready o_t os_ready out_done""".split()
        S = {n: sem(n) for n in names}
        for k in ("1", "2"):
            for n in ("mean", "delta", "square", "var", "vareps", "rstd", "rstd_tr", "rstd_row", "rstd_bc", "x"):
                S[n + k] = sem(n + k)

        GS, GB, OS, OB, BT, CL = vec[:, 0:4], vec[:, 4:8], vec[:, 8:9], vec[:, 9:10], vec[:, 10:11], vec[:, 11:12]
        V2 = lambda t: t[:, 0:T2]
        block = ctx.enter_context(nc.Block())

        def turn(attend, mlp, end, n, late, early):
            f, ahead, w = AHEAD, 0, NF - LAG
            for s in SCHEDULE:
                if s == "c":
                    if n is not None:
                        mlp(f, n)
                    f += 1
                elif s == "a":
                    if late is not None:
                        mlp(ahead, late)
                    ahead += 1
                elif s in OUTPUT:
                    if n is not None:
                        end(s, n, w)
                    w += s == "w2t"
                elif s in EARLY:
                    if early is not None:
                        attend(s, early)
                elif late is not None:
                    attend(s, late)

        def turns(eng, attend, mlp, end, setup=lambda: None):
            for s in EARLY:
                attend(s, 0)
            setup()
            turn(attend, mlp, end, None, 0, 1)
            with eng.Fori(0, PAIRS - 2) as n:
                turn(attend, mlp, end, n, n + 1, n + 2)
            turn(attend, mlp, end, PAIRS - 2, PAIRS - 1, None)
            turn(attend, mlp, end, PAIRS - 1, None, None)

        def ring_wait(eng, sem_, f, n):
            if f >= RING or not is_first(n):
                eng.wait_ge(sem_, n * NF + f - RING + 1)

        @block.sync
        def _(sp):
            loads = [(con[:, :], consts), (wq_z[:, 64:128], wq), (wk_z[:, 64:128], wk), (wv_s[:, :], wv),
                     (GS, gn_in[:, 0:4]), (GB, gn_in[:, 4:8]), (vec[:, 8:10], gn_out), (BT, b_tok), (CL, cls),
                     (pos_s[:, :], pos), (wg_s[:, :], wg), (b1_s[:, :], b1), (b2_s[:, :], b2),
                     (w2_s[:, :, :], w2), (rv[:, :], rel_v)]
            for dst, src in loads:
                sp.dma_start(dst, src).then_inc(S["const_in"], 16)
            for r in range(8):
                a = 126 - r
                sp.dma_start(t1[r:P - 7 + r:8, 0:2 * L - 1], rel_rev[:, a:a + 2 * L - 1]).then_inc(S["const_in"], 16)
            def tokens(t):
                sp.dma_start(tok[:, :, :], tok_scratch[:, bass.ds(t * 2, 2), :]).then_inc(S["tok_in"], 16)
                sp.dma_start(txt_s[:, :, :], txt[bass.ds(t * 2, 2), :, :].rearrange("b t c -> t b c")).then_inc(S["tok_in"], 16)

            def store(n):
                sp.wait_ge(S["os_ready"], n * 2 + 4)
                for k, (a, w) in enumerate(GT):
                    sp.dma_start(out[bass.ds(n * T2 + a, w), :], o_s[0:w, k, :]).then_inc(S["out_done"], 16)

            tokens(0)
            for piece in range(2):
                if piece:
                    sp.wait_ge(S["w1_split"], 2)
                sp.dma_start(w1_st.rearrange("d (e f) -> d e f", f=FF),
                             w1[4 * piece:4 * piece + 4, :, :].rearrange("e d f -> d e f")).then_inc(S["w1_in"], 16)

            for t in range(2):
                sp.wait_ge(S["h_ready"], t * 2 + 2)
                tokens(t + 1)
            with sp.Fori(0, PAIRS - 3) as n:
                sp.wait_ge(S["h_ready"], n * 2 + 6)
                tokens(n + 3)
                store(n)
            store(PAIRS - 3)
            store(PAIRS - 2)
            store(PAIRS - 1)
            sp.wait_ge(S["out_done"], 64 * PAIRS + 64)

        N_CONST = 16 * (15 + 8)

        @block.tensor
        def _(pe):
            mm = nc.tensor.matmul

            def w2_step(f, n):
                if f == 0:
                    pe.wait_ge(S["os_ready"], n * 2 + 2)
                pe.wait_ge(S["hs_done"], n * NF + f + 1)
                mm(yb[:, 0:T2], w2_s[:, f, :], gelu1[:, f % RING, :], start=(f == 0), stop=(f == NF - 1)).then_inc(S["w2_done"], 1)

            def mlp(f, n):
                if f == 0:
                    pe.wait_ge(S["xh_done"], n + 1)
                if f >= 2 or not is_first(n):
                    pe.wait_ge(S["g_done"], n * (2 * NF) + 2 * (f - 2) + 1)
                z = zb[f % 2][:, 0:T2]
                w = slice(f * P, (f + 1) * P)
                mm(z, w1_hi[:, w], x_hi[:, :], start=True, stop=False)
                mm(z, w1_lo[:, w], x_hi[:, :], start=False, stop=False)
                if f == 0:
                    pe.wait_ge(S["ffn_in"], n * 2 + 2)
                mm(z, w1_hi[:, w], x_lo[:, :], start=False, stop=True).then_inc(S["z_ready"], 1)
                if f >= LAG:
                    w2_step(f - LAG, n)

            def end(s, n, f):
                if s == "w2t":
                    w2_step(f, n)
                elif s == "otr":
                    pe.wait_ge(S["ot_ready"], n + 1)
                    for k, (a, w) in enumerate(GT):
                        i = nc.tensor.transpose(yb[0:w, k * P:(k + 1) * P], hres[:, a:a + w], ident)
                    i.then_inc(S["o_t"], 1)

            def mean_of(k, t):
                pe.wait_ge(S["h_ready" if k == "1" else "h2_ready"], t * 2 + 2)
                src = h[:, :, :].rearrange("p b l -> p (b l)") if k == "1" else h2[:, :]
                mm(LN[k][0][:, 0:T2], ones, src, start=True, stop=True).then_inc(S["mean" + k], 1)

            def var_of(k, t):
                ps, _, sq, _, _ = LN[k]
                pe.wait_ge(S["square" + k], t + 1)
                for i, a in enumerate(GO):
                    m = mm(ps[0:GW, i:i + 1], sq[:, a:a + GW], ones[:, 0:1], start=True, stop=True)
                m.then_inc(S["var" + k], 1)

            def broadcast(ps, rows, first, src):
                for i, a in enumerate(GO):
                    m = mm(ps[:, a:a + GW], ident[0:rows, first + i:first + i + 1].broadcast_to([rows, P]), src,
                           start=True, stop=True)
                return m

            def transpose_v(b, t):
                if b == 0:
                    pe.wait_ge(S["norm"], t * 6 + 6)
                for c, (j0, jn) in enumerate(JC):
                    i = nc.tensor.transpose(misc[0:jn, c * P:(c + 1) * P], e2[:, b * L + j0:b * L + j0 + jn], ident)
                i.then_inc(S["vt"], 1)

            def attend(s, t):
                if s == "txt":
                    pe.wait_ge(S["tok_in"], t * 32 + 32)
                    if not is_first(t):
                        pe.wait_ge(S["v_copied"], t * 4)
                    for b in range(2):
                        i = nc.tensor.transpose(misc[:, b * P:(b + 1) * P], txt_s[:, b, :], ident)
                    i.then_inc(S["txt_t"], 1)
                elif s in ("mean1", "mean2"):
                    mean_of(s[4], t)
                elif s in ("var1", "var2"):
                    var_of(s[3], t)
                elif s in ("inv1", "inv2"):
                    pe.wait_ge(S["rstd" + s[3]], t + 1)
                    ps, _, _, rs, _ = LN[s[3]]
                    nc.tensor.transpose(ps[0:4, 0:GW], rs[0:GW, 0:4], ident[0:GW, 0:GW]).then_inc(S["rstd_tr" + s[3]], 1)
                elif s in ("bc1", "bc2"):
                    pe.wait_ge(S["rstd_row" + s[2]], t + 1)
                    ps, _, _, _, rs_t = LN[s[2]]
                    broadcast(ps, 4, 0, rs_t[:, :]).then_inc(S["rstd_bc" + s[2]], 1)
                elif s == "proj":
                    pe.wait_ge(S["x1"], t + 1)
                    for wz, c0 in ((wq_z, 0), (wk_z, 256)):
                        for b in range(2):
                            i = mm(misc[:, c0:c0 + L], wz[:, 64 - 64 * b:192 - 64 * b], e2[:, b * L:(b + 1) * L],
                                   start=(b == 0), stop=(b == 1))
                    i.then_inc(S["qk_ready"], 1)
                    mm(lg[0][:, 0:T2], wv_s[:, :], V2(e2), start=True, stop=True).then_inc(S["v_ready"], 1)
                elif s == "gmean":
                    pe.wait_ge(S["mv_ready"], t * 4 + 4)
                    mm(lg[1][:, 0:4], g8, mv[:, :, 0], start=True, stop=True).then_inc(S["gmean"], 1)
                elif s == "gvar":
                    pe.wait_ge(S["gspread"], t + 1)
                    mm(lg[1][:, 0:4], g8, gst[:, 3, :], start=True, stop=True).then_inc(S["gvar"], 1)
                elif s[:3] == "sel":
                    part = int(s[3])
                    k_x, q_x = (k_hi, q_hi) if part < 4 else (k_lo, q_lo)
                    if part == 0:
                        pe.wait_ge(S["norm"], t * 6 + 6)
                    if part == 4:
                        pe.wait_ge(S["lo"], t * 2 + 2)
                    for i in range(2 * part, 2 * part + 2):
                        if i >= 2:
                            pe.wait_ge(S["sel_done"], t * 16 + i - 1)
                        for k in range(2):
                            bh = 2 * (i % 8) + k
                            dst = lg[i % 2][:, k * 256:k * 256 + LP]
                            for z, x in ((0, k_x), (1, q_x)):
                                c0 = 64 - 64 * z + P * bh
                                m = mm(dst, sel_z[:, c0:c0 + P], x[:, :], start=(z == 0), stop=(z == 1))
                        m.then_inc(S["sel_ready"], 1)
                elif s == "vt0":
                    transpose_v(0, t)
                elif s[:3] == "max":
                    if s == "max0":
                        pe.wait_ge(S["q_spread"], t * 4 + 2)
                    for i in MAX_FILLS[s]:
                        pe.wait_ge(S["sel_done"], t * 16 + 15 + i) if i < 2 else pe.wait_ge(S["max_done"], t * 13 + i - 1)
                        for k in range(2 if 2 * i + 1 < OCT else 1):
                            o = 2 * i + k
                            dst = lg[i % 2][:, k * 256:k * 256 + L + 1]
                            mm(dst, q_bd[0][:, o, :, :], k_hi[:, 0:L + 1], start=True, stop=False)
                            m = mm(dst, a_bd[0][:, o, :, :], rw_hi[:, 192 - 8 * o:192 - 8 * o + L + 1], start=False, stop=True)
                        m.then_inc(S["max_ready"], 1)
                elif s == "mrow":
                    pe.wait_ge(S["max_done"], t * 13 + 13)
                    pe.wait_ge(S["v_copied"], t * 4 + 2)
                    nc.tensor.transpose(misc[0:OCT, 0:P], mx[:, 0:OCT], ident).then_inc(S["mx_t"], 1)
                elif s == "vt1":
                    pe.wait_ge(S["mt_ready"], t + 1)
                    transpose_v(1, t)
                elif s == "scores":
                    pe.wait_ge(S["q_spread"], t * 4 + 4)
                    i = 0
                    for g in range(NG):
                        octs = range(g * GRP, min(OCT, (g + 1) * GRP))
                        for c, (j0, jn) in enumerate(JC):
                            pe.wait_ge(S["max_done"], t * 13 + 12 + i) if i < 2 else pe.wait_ge(S["exp_done"], t * 14 + i - 1)
                            ps = lg[(1 + i) % 2]
                            whole = ps[0:jn, 0:len(octs) * P]
                            js = slice(j0, j0 + jn)
                            os_ = slice(octs[0], octs[-1] + 1)
                            mm(whole, k_hi[:, js], q_bd[0][:, os_, :, :], start=True, stop=False)
                            mm(whole, k_lo[:, js], q_bd[0][:, os_, :, :], start=False, stop=False)
                            mm(whole, k_hi[:, js], q_bd[1][:, os_, :, :], start=False, stop=False)
                            for o in octs:
                                part = ps[0:jn, (o - octs[0]) * P:(o - octs[0] + 1) * P]
                                win = slice(192 - 8 * o + j0, 192 - 8 * o + j0 + jn)
                                mm(part, rw_hi[:, win], a_bd[0][:, o, :, :], start=False, stop=False)
                                mm(part, rw_lo[:, win], a_bd[0][:, o, :, :], start=False, stop=False)
                                mm(part, rw_hi[:, win], a_bd[1][:, o, :, :], start=False, stop=False)
                                m = mm(part, pick_o[0:32 + OCT, o:o + 1].broadcast_to([32 + OCT, jn]), mt[0:32 + OCT, :],
                                       start=False, stop=(o == octs[-1]))
                            m.then_inc(S["scores"], 1)
                            i += 1
                elif s in ("pv0", "pv1"):
                    b = int(s[2])
                    pe.wait_ge(S["exp_done"], t * 14 + 14)
                    pe.wait_ge(S["v_copied"], t * 4 + 2 + 2 * b)
                    for hh in range(H):
                        for c, (j0, jn) in enumerate(JC):
                            m = mm(pv[b][:, hh // 4 * 256:hh // 4 * 256 + LP], v_pad[0:jn, c, hh, :],
                                   pr[c][0:jn, :, H * b + hh, :], start=(hh == 0 and c == 0), stop=False,
                                   skip_group_check=True)
                    m.then_inc(S["pv_done"], 1)
                elif s == "rel":
                    for g in range(NG):
                        octs = range(g * GRP, min(OCT, (g + 1) * GRP))
                        if g >= 2:
                            pe.wait_ge(S["wm_done"], t * NG + g - 1)
                        ps = lg[(1 + g) % 2]
                        for o in octs:
                            part = ps[:, (o - octs[0]) * P:(o - octs[0] + 1) * P]
                            mm(part, rv[:, (8 * o + P) * HD:(8 * o + P) * HD + P], pr[0][:, o, :, :], start=True, stop=False)
                            m = mm(part, rv[0:JC[1][1], 8 * o * HD:8 * o * HD + P], pr[1][0:JC[1][1], o, :, :],
                                   start=False, stop=True)
                        m.then_inc(S["rel_ready"], 1)
                elif s in ("place0", "place1"):
                    b = int(s[5])
                    pe.wait_ge(S["wm_done"], t * NG + NG)
                    for hh in range(H):
                        m = mm(pv[b][:, hh // 4 * 256:hh // 4 * 256 + LP], K["place"][:, 112 - 16 * hh:112 - 16 * hh + P],
                               pr[0][:, :, H * b + hh, :], start=False, stop=(hh == H - 1), skip_group_check=True)
                    m.then_inc(S["pv_ready"], 1)
                elif s == "omean":
                    pe.wait_ge(S["omv"], t * 2 + 2)
                    mm(pv[0][:, 0:2], g4, mv_o[:, :, 0], start=True, stop=True).then_inc(S["omean"], 1)
                elif s == "ovar":
                    pe.wait_ge(S["ospread"], t + 1)
                    mm(pv[0][:, 0:2], g4, gst_o[:, 3, 0:2], start=True, stop=True).then_inc(S["ovar"], 1)
                elif s == "gate":
                    pe.wait_ge(S["x2"], t + 1)
                    for k, a in enumerate(GO):
                        m = mm(pv[0][0:GW, 8 * k:8 * k + 8], t2[:, a:a + GW], wg_s[:, :], start=True, stop=True)
                    m.then_inc(S["logits"], 1)
                elif s == "top":
                    pe.wait_ge(S["p1_ready"], t + 1)
                    nc.tensor.transpose(pv[0][0:8, 0:GW], ep[0:GW, :], ident[0:GW, 0:GW]).then_inc(S["ep_tr"], 1)
                elif s == "bcast":
                    pe.wait_ge(S["ep_copied"], t + 1)
                    broadcast(pv[0], 8, 0, ep_t[:, :])
                    broadcast(pv[1], 8, 4, ep_t[:, :]).then_inc(S["bcast_ready"], 1)

            pe.wait_ge(S["const_in"], N_CONST)
            pe.wait_ge(S["setup_dve"], 15)
            turns(pe, attend, mlp, end, lambda: pe.wait_ge(S["w1_split"], 4))

        @block.vector
        def _(dve):
            v = nc.vector

            def carry_wait(k):
                v.memset(wait_slot[:, k:k + 1], 0.0)

            def mlp(f, n):
                dve.wait_ge(S["z_ready"], n * NF + f + 1)
                ring_wait(dve, S["hs_done"], f, n)
                v.tensor_tensor(gelu2[:, f % RING, :], zb[f % 2][:, 0:T2], ratio[:, :], ALU.mult).then_inc(S["z2_done"], 1)

            def end(s, n, _f):
                if s == "otr":
                    dve.wait_ge(S["w2_done"], n * NF + NF)
                    dve.wait_ge(S["hres_done"], n + 1)
                    v.tensor_tensor(hres[:, :], yb[:, 0:T2], hres[:, :], ALU.add).then_inc(S["ot_ready"], 1)
                elif s == "ocopy":
                    dve.wait_ge(S["o_t"], n + 1)
                    dve.wait_ge(S["out_done"], n * 64 + 64)
                    v.tensor_copy(o_s[0:GW, 0:2, :], yb[0:GW, 0:2 * P].rearrange("p (k c) -> p k c", k=2)).then_inc(S["os_ready"], 1)
                    v.tensor_copy(o_s[0:96, 2:4, :], yb[0:96, 2 * P:4 * P].rearrange("p (k c) -> p k c", k=2)).then_inc(S["os_ready"], 1)

            def layernorm(s, k, t):
                src = h[:, :, :].rearrange("p b l -> p (b l)") if k == "1" else h2[:, :]
                ps, delta, sq, rs, rs_t = LN[k]
                if s == "mean":
                    dve.wait_ge(S["mean" + k], t + 1)
                    v.tensor_tensor(V2(delta), src, ps[:, 0:T2], ALU.subtract).then_inc(S["delta" + k], 1)
                    dve.wait_ge(S["delta" + k], t + 1)
                    v.tensor_tensor(V2(sq), V2(delta), V2(delta), ALU.mult).then_inc(S["square" + k], 1)
                elif s == "var":
                    dve.wait_ge(S["var" + k], t + 1)
                    v.tensor_scalar(rs[0:GW, 0:4], ps[0:GW, 0:4], LN_EPS, None, ALU.add).then_inc(S["vareps" + k], 1)
                elif s == "inv":
                    dve.wait_ge(S["rstd_tr" + k], t + 1)
                    v.tensor_copy(rs_t[:, :], ps[0:4, 0:GW]).then_inc(S["rstd_row" + k], 1)
                else:
                    dve.wait_ge(S["rstd_bc" + k], t + 1)
                    v.tensor_tensor(V2(sq), V2(delta), ps[:, 0:T2], ALU.mult).then_inc(S["x" + k], 1)

            def group_spread(m, stats, gs, psum, ready, tmp, done, t):
                gm, dm, d2, spread = (gs[:, i, 0:m] for i in range(4))
                dve.wait_ge(ready, t + 1)
                v.tensor_copy(gm, psum)
                v.tensor_tensor(dm, stats[:, 0:m, 0], psum, ALU.subtract).then_inc(tmp, 1)
                dve.wait_ge(tmp, t * 2 + 1)
                v.tensor_tensor(d2, dm, dm, ALU.mult).then_inc(tmp, 1)
                dve.wait_ge(tmp, t * 2 + 2)
                v.tensor_tensor(spread, d2, stats[:, 0:m, 1], ALU.add).then_inc(done, 1)

            def group_affine(m, gs, rstd, part, done, scale, bias, t):
                gm, _, d2, _, rs, sc, bi = (gs[:, i, 0:m] for i in range(7))
                dve.wait_ge(rstd, t + 1)
                v.tensor_tensor(sc, scale, rs, ALU.mult).then_inc(part, 1)
                dve.wait_ge(part, t * 2 + 1)
                v.tensor_tensor(d2, gm, sc, ALU.mult).then_inc(part, 1)
                dve.wait_ge(part, t * 2 + 2)
                v.tensor_tensor(bi, bias, d2, ALU.subtract).then_inc(done, 1)

            def attend(s, t):
                if s == "txt":
                    dve.wait_ge(S["tok_in"], t * 32 + 32)
                    if not is_first(t):
                        dve.wait_ge(S["h_kept"], t)
                    v.scalar_tensor_tensor(out=h[:, :, 1:1 + NPATCH], in0=tok[:, :, :], scalar=BT,
                                           in1=pos_s[:, 1:].unsqueeze(1).broadcast_to([P, 2, NPATCH]),
                                           op0=ALU.add, op1=ALU.mult).then_inc(S["h_ready"], 1)
                    dve.wait_ge(S["txt_t"], t + 1)
                    v.tensor_copy(h[:, :, 1 + NPATCH:], misc[:, 0:2 * P].rearrange("p (b l) -> p b l", b=2)).then_inc(S["h_ready"], 1)
                elif s in ("mean1", "mean2"):
                    layernorm("mean", s[4], t)
                elif s in ("var1", "var2"):
                    layernorm("var", s[3], t)
                elif s in ("inv1", "inv2"):
                    layernorm("inv", s[3], t)
                elif s in ("bc1", "bc2"):
                    layernorm("bc", s[2], t)
                elif s == "proj":
                    dve.wait_ge(S["qk_ready"], t + 1)
                    v.bn_stats(st[:, 0, :], misc[:, 0:L]).then_inc(S["bn"], 1)
                    v.bn_stats(st[:, 1, :], misc[:, 256:256 + L]).then_inc(S["bn"], 1)
                    dve.wait_ge(S["v_ready"], t + 1)
                    for b in range(2):
                        v.bn_stats(st[:, 2 + b, :], lg[0][:, b * L:(b + 1) * L]).then_inc(S["bn"], 1)
                    dve.wait_ge(S["bn"], t * 4 + 4)
                    carry_wait(0)
                    for k in range(4):
                        v.bn_aggr(mv[:, k, :], st[:, k, :]).then_inc(S["mv_ready"], 1)
                elif s == "gmean":
                    group_spread(4, mv, gst, lg[1][:, 0:4], S["gmean"], S["gtmp"], S["gspread"], t)
                elif s == "gvar":
                    dve.wait_ge(S["gvar"], t + 1)
                    v.tensor_scalar(gst[:, 4, :], lg[1][:, 0:4], GN_EPS, None, ALU.add).then_inc(S["gve"], 1)
                elif s == "gaff":
                    group_affine(4, gst, S["grstd"], S["affine_part"], S["affine"], GS, GB, t)
                elif s == "glo":
                    dve.wait_ge(S["norm"], t * 6 + 4)
                    for x, lo, hi in ((e1[:, 0:L], q_lo, q_hi), (e1[:, LP:LP + L], k_lo, k_hi)):
                        v.tensor_tensor(lo[:, 0:L], x, hi[:, 0:L].bitcast(F32), ALU.subtract).then_inc(S["lo"], 1)
                elif s[:3] == "sel":
                    part = int(s[3])
                    for i in range(2 * part, 2 * part + 2):
                        bh = 2 * (i % 8)
                        dve.wait_ge(S["sel_ready"], t * 16 + i + 1)
                        v.tensor_tensor(a_bd[i // 8][:, :, bh:bh + 2, :].rearrange("p o b r -> p b o r"),
                                        lg[i % 2][:, :].rearrange("p (b x) -> p b x", b=2)[:, :, 0:LP].rearrange("p b (o r) -> p b o r", r=8),
                                        K["mask_q"].unsqueeze(1).unsqueeze(1).broadcast_to([P, 2, OCT, 8]),
                                        ALU.mult).then_inc(S["sel_done"], 1)
                elif s[:3] == "max":
                    for i in MAX_FILLS[s]:
                        dve.wait_ge(S["max_ready"], t * 13 + i + 1)
                        w = 2 if 2 * i + 1 < OCT else 1
                        v.tensor_reduce(mx[:, 2 * i:2 * i + w], lg[i % 2][:, :].rearrange("p (k x) -> p k x", k=2)[:, 0:w, 0:L],
                                        AX, ALU.max).then_inc(S["max_done"], 1)
                elif s == "mrow":
                    dve.wait_ge(S["mx_t"], t + 1)
                    v.tensor_scalar(mt[0:OCT, :], misc[0:OCT, 0:P], -1.0, None, ALU.mult).then_inc(S["mt_hi"], 1)
                    dve.wait_ge(S["mt_hi"], t + 1)
                    v.scalar_tensor_tensor(out=mt[32:32 + OCT, :], in0=misc[0:OCT, 0:P], scalar=-1.0, in1=mt[0:OCT, :],
                                           op0=ALU.mult, op1=ALU.subtract).then_inc(S["mt_ready"], 1)
                elif s == "rel":
                    for g in range(NG):
                        w = min(OCT, (g + 1) * GRP) - g * GRP
                        dve.wait_ge(S["rel_ready"], t * NG + g + 1)
                        v.tensor_tensor(pr[0][:, g * GRP:g * GRP + w, :, :].rearrange("p o b r -> p (o b) r"),
                                        lg[(1 + g) % 2][:, 0:w * P].rearrange("p (x r) -> p x r", r=8),
                                        K["mask_r"].unsqueeze(1).broadcast_to([P, w * BH, 8]), ALU.mult).then_inc(S["wm_done"], 1)
                elif s in ("place0", "place1"):
                    b = int(s[5])
                    bs = slice(b * L, (b + 1) * L)
                    dve.wait_ge(S["pv_ready"], t * 2 + b + 1)
                    halves = ((0, 0, 64), (256, 64, 0))
                    for a, n_, d_ in halves:
                        v.reciprocal(t2[n_:n_ + 64, bs], pv[b][d_:d_ + 64, a:a + L]).then_inc(S["rec_done"], 1)
                    for k, (a, n_, _) in enumerate(halves):
                        dve.wait_ge(S["rec_done"], t * 4 + 2 * b + k + 1)
                        v.tensor_tensor(t1[n_:n_ + 64, bs], pv[b][n_:n_ + 64, a:a + L], t2[n_:n_ + 64, bs],
                                        ALU.mult).then_inc(S["o_part"], 1)
                    dve.wait_ge(S["o_part"], t * 4 + 2 * b + 2)
                    v.bn_stats(st_o[:, b, :], t1[:, bs]).then_inc(S["obn"], 1)
                    dve.wait_ge(S["obn"], t * 2 + b + 1)
                    carry_wait(1 + b)
                    v.bn_aggr(mv_o[:, b, :], st_o[:, b, :]).then_inc(S["omv"], 1)
                elif s == "omean":
                    group_spread(2, mv_o, gst_o, pv[0][:, 0:2], S["omean"], S["otmp"], S["ospread"], t)
                elif s == "ovar":
                    dve.wait_ge(S["ovar"], t + 1)
                    v.tensor_scalar(gst_o[:, 4, 0:2], pv[0][:, 0:2], GN_EPS, None, ALU.add).then_inc(S["ove"], 1)
                elif s == "oaff":
                    group_affine(2, gst_o, S["orstd"], S["oaff_part"], S["oaffine"],
                                 OS.broadcast_to([P, 2]), OB.broadcast_to([P, 2]), t)
                elif s == "oh2":
                    for b in range(2):
                        dve.wait_ge(S["onorm"], t * 2 + b + 1)
                        bs = slice(b * L, (b + 1) * L)
                        v.tensor_tensor(h2[:, bs], h2[:, bs], t2[:, bs], ALU.add).then_inc(S["h2_ready"], 1)
                elif s == "gate":
                    dve.wait_ge(S["logits"], t + 1)
                    carry_wait(3)
                    for k in range(4):
                        v.max(top8[0:GW, k, :], pv[0][0:GW, 8 * k:8 * k + 8]).then_inc(S["top_done"], 1)
                    dve.wait_ge(S["top_done"], t * 4 + 4)
                    v.tensor_tensor(dl[0:GW, 0:4], top8[0:GW, :, 1], top8[0:GW, :, 0], ALU.subtract).then_inc(S["dl_ready"], 1)
                elif s == "gate2":
                    dve.wait_ge(S["e_ready"], t + 1)
                    v.tensor_scalar(dl[0:GW, 4:8], ep[0:GW, 0:4], 1.0, None, ALU.add).then_inc(S["e1_ready"], 1)
                    dve.wait_ge(S["e1_ready"], t + 1)
                    v.reciprocal(ep[0:GW, 4:8], dl[0:GW, 4:8]).then_inc(S["p1_ready"], 1)
                elif s == "top":
                    dve.wait_ge(S["ep_tr"], t + 1)
                    v.tensor_copy(ep_t[:, 0:GW], pv[0][0:8, 0:GW]).then_inc(S["ep_copied"], 1)
                elif s == "bcast":
                    dve.wait_ge(S["bcast_ready"], t + 1)
                    v.tensor_tensor(V2(t1), V2(t2), pv[1][:, 0:T2], ALU.mult).then_inc(S["xp_done"], 1)
                elif s == "xin":
                    if not is_first(t):
                        dve.wait_ge(S["z2_done"], t * NF)
                    v.tensor_copy(ratio[:, :], pv[0][:, 0:T2]).then_inc(S["ffn_in"], 1)
                    dve.wait_ge(S["xh_done"], t + 1)
                    v.tensor_tensor(x_lo[:, :], V2(t1), x_hi[:, :].bitcast(F32), ALU.subtract).then_inc(S["ffn_in"], 1)
                elif s == "hres":
                    if not is_first(t):
                        dve.wait_ge(S["o_t"], t)
                    v.tensor_scalar(hres[:, :], h2[:, :], b2x2[:, :], None, ALU.add).then_inc(S["hres_done"], 1)

            z = S["setup_dve"]
            v.memset(wq_z[:, 0:64], 0.0); v.memset(wq_z[:, 128:192], 0.0)
            v.memset(wk_z[:, 0:64], 0.0); v.memset(wk_z[:, 128:192], 0.0)
            v.memset(mt[:, :], 0.0)
            for x in (q_hi, q_lo, k_hi, k_lo):
                v.memset(x[:, :].bitcast(F32), 0.0).then_inc(z, 1)
            v.memset(half[:, 0:1], -0.5).then_inc(z, 1)
            v.memset(half[:, 1:2], 2.718281828459045).then_inc(z, 1)
            v.memset(v_pad[:, :, :, :], 0.0).then_inc(z, 1)
            v.memset(sel_z[:, :].bitcast(F32), 0.0).then_inc(z, 1)
            dve.wait_ge(z, 8)
            for hh in range(H):
                c0 = (64 if hh < 4 else 0) + (hh % 4) * HD
                last = v.memset(v_pad[:, :, hh, c0:c0 + HD], 1.0)
            last.then_inc(z, 1)
            dve.wait_ge(S["const_in"], N_CONST)
            v.memset(t1[:, 2 * L - 1:2 * L], 0.0).then_inc(z, 1)
            v.tensor_copy(pick_o[0:32, :], con[0:32, 0:32])
            v.tensor_copy(pick_o[32:64, :], con[0:32, 0:32])
            v.tensor_tensor(sel_z[:, 64:].rearrange("p (b z e r) -> p b z e r", b=BH, z=2, e=8)[:, :, 0, :, :],
                            K["mask_bh"].unsqueeze(2).unsqueeze(3).broadcast_to([P, BH, 8, 8]),
                            K["mask_q"].unsqueeze(1).unsqueeze(3).broadcast_to([P, BH, 8, 8]), ALU.mult)
            for b in range(2):
                v.tensor_tensor(h[:, b, 0:1], CL, pos_s[:, 0:1], ALU.mult)
            v.tensor_reduce(b2x2[:, :], b2_s[:, :], AX, ALU.add).then_inc(z, 1)
            dve.wait_ge(z, 11)
            v.tensor_scalar(b2x2[:, :], b2x2[:, :], 2.0, None, ALU.mult).then_inc(z, 1)
            v.tensor_copy(rw_hi[:, :], V2(t1)).then_inc(z, 1)
            dve.wait_ge(z, 13)
            v.tensor_tensor(rw_lo[:, :], V2(t1), rw_hi[:, :].bitcast(F32), ALU.subtract).then_inc(z, 2)
            dve.sem_inc(S["out_done"], 64)
            dve.sem_inc(S["os_ready"], 2)

            def split_w1():
                for piece in range(2):
                    dve.wait_ge(S["w1_in"], 16 * piece + 16)
                    a = slice(2048 * piece, 2048 * piece + 2048)
                    v.tensor_copy(w1_hi[:, a], w1_st).then_inc(S["w1_split"], 1)
                    dve.wait_ge(S["w1_split"], 2 * piece + 1)
                    v.tensor_tensor(w1_lo[:, a], w1_st, w1_hi[:, a].bitcast(F32), ALU.subtract).then_inc(S["w1_split"], 1)

            turns(dve, attend, mlp, end, split_w1)

        @block.scalar
        def _(act):
            a = nc.scalar.activation

            def mlp(f, n):
                act.wait_ge(S["z2_done"], n * NF + f + 1)
                ring_wait(act, S["w2_done"], f, n)
                a(gelu1[:, f % RING, :], zb[f % 2][:, 0:T2], ACT.Gelu, bias=b1_s[:, f:f + 1]).then_inc(S["g_done"], 1)
                a(gelu2[:, f % RING, :], gelu2[:, f % RING, :], ACT.Gelu, bias=b1_s[:, f:f + 1]).then_inc(S["g_done"], 1)

            def copy_v(b, t):
                act.wait_ge(S["vt"], t * 2 + b + 1)
                if b == 1:
                    act.wait_ge(S["pv_done"], t * 2 + 1)
                for c, (j0, jn) in enumerate(JC):
                    blk = v_pad[0:jn, c, :, :].rearrange("p h n -> p (h n)")
                    dst = bass.AP(tensor=blk.tensor, offset=blk.offset, ap=[list(blk.ap[0]), [P + HD, H], [1, HD]])
                    a(dst, misc[0:jn, c * P:(c + 1) * P].rearrange("p (h d) -> p h d", h=H), ACT.Copy).then_inc(S["v_copied"], 1)

            def attend(s, t):
                if s == "gaff":
                    act.wait_ge(S["affine"], t + 1)
                    sc, bi = gst[:, 5, :], gst[:, 6, :]
                    for k, ps, hi, val in ((0, misc[:, 0:L], q_hi[:, 0:L], e1[:, 0:L]),
                                           (1, misc[:, 256:256 + L], k_hi[:, 0:L], e1[:, LP:LP + L])):
                        for dst in (hi, val):
                            a(dst, ps, ACT.Identity, bias=bi[:, k:k + 1], scale=sc[:, k:k + 1]).then_inc(S["norm"], 1)
                    for b in range(2):
                        a(e2[:, b * L:(b + 1) * L], lg[0][:, b * L:(b + 1) * L], ACT.Identity,
                          bias=bi[:, 2 + b:3 + b], scale=sc[:, 2 + b:3 + b]).then_inc(S["norm"], 1)
                elif s == "vt0":
                    copy_v(0, t)
                elif s == "hkeep":
                    if not is_first(t):
                        act.wait_ge(S["hres_done"], t)
                    a(h2[:, :], h[:, :, :].rearrange("p b l -> p (b l)"), ACT.Copy).then_inc(S["h_kept"], 1)
                elif s == "scores":
                    i = 0
                    for g in range(NG):
                        w = min(OCT, (g + 1) * GRP) - g * GRP
                        for c, (j0, jn) in enumerate(JC):
                            act.wait_ge(S["scores"], t * 14 + i + 1)
                            a(pr[c][0:jn, g * GRP:g * GRP + w, :, :].rearrange("p o b r -> p (o b r)"),
                              lg[(1 + i) % 2][0:jn, 0:w * P], ACT.Exp).then_inc(S["exp_done"], 1)
                            i += 1
                elif s == "pv0":
                    copy_v(1, t)
                elif s == "oaff":
                    act.wait_ge(S["oaffine"], t + 1)
                    for b in range(2):
                        bs = slice(b * L, (b + 1) * L)
                        a(t2[:, bs], t1[:, bs], ACT.Identity, bias=gst_o[:, 6, b:b + 1], scale=gst_o[:, 5, b:b + 1]).then_inc(S["onorm"], 1)
                elif s == "xin":
                    act.wait_ge(S["xp_done"], t + 1)
                    a(x_hi[:, :], V2(t1), ACT.Copy).then_inc(S["xh_done"], 1)

            act.wait_ge(S["setup_dve"], 9)
            act.wait_ge(S["const_in"], N_CONST)
            turns(act, attend, mlp, lambda s, n, f: None)

        @block.gpsimd
        def _(pool):
            g = nc.gpsimd

            def mlp(f, n):
                pool.wait_ge(S["g_done"], n * (2 * NF) + 2 * f + 2)
                g.tensor_tensor(gelu1[:, f % RING, :], gelu1[:, f % RING, :], gelu2[:, f % RING, :], ALU.add).then_inc(S["hs_done"], 1)

            def rsqrt(x, ready, done, t):
                pool.wait_ge(ready, t + 1)
                g.tensor_tensor(x, x, half[0:x.shape[0], 0:1].broadcast_to(list(x.shape)), ALU.pow).then_inc(done, 1)

            def attend(s, t):
                if s in ("var1", "var2"):
                    rsqrt(LN[s[3]][3][0:GW, 0:4], S["vareps" + s[3]], S["rstd" + s[3]], t)
                elif s == "gvar":
                    rsqrt(gst[:, 4, :], S["gve"], S["grstd"], t)
                elif s == "ovar":
                    rsqrt(gst_o[:, 4, 0:2], S["ove"], S["orstd"], t)
                elif s[:2] == "qs":
                    k, part = divmod(int(s[2]), 2)
                    x = (q_hi, q_lo)[k]
                    if k == 0:
                        pool.wait_ge(S["norm"], t * 6 + 4)
                    else:
                        pool.wait_ge(S["lo"], t * 2 + 2)
                    o0, on = ((0, 13), (13, OCT - 13))[part]
                    g.tensor_tensor(q_bd[k][:, o0:o0 + on, :, :],
                                    x[:, 8 * o0:8 * (o0 + on)].bitcast(F32).rearrange("p (o r) -> p o r", r=8).unsqueeze(2).broadcast_to([P, on, BH, 8]),
                                    K["mask_bh"].unsqueeze(1).unsqueeze(3).broadcast_to([P, on, BH, 8]), ALU.mult).then_inc(S["q_spread"], 1)
                elif s == "gate":
                    pool.wait_ge(S["dl_ready"], t + 1)
                    g.tensor_tensor(ep[0:GW, 0:4], half[0:GW, 1:2].broadcast_to([GW, 4]), dl[0:GW, 0:4], ALU.pow).then_inc(S["e_ready"], 1)

            pool.wait_ge(S["setup_dve"], 9)
            pool.wait_ge(S["const_in"], N_CONST)
            turns(pool, attend, mlp, lambda s, n, f: None)


def build(nc, a, out):
    tok_scratch = nc.dram_tensor("tok_scratch", (P, B, NPATCH), F32, kind="Internal").ap()
    patch_embed(nc, a["x"], a["w_tok"], tok_scratch)
    fused_block(nc, a["txt"], a["b_tok"], a["cls"], a["pos"], a["wq"], a["wk"], a["wv"], a["gn_in"], a["rel_rev"],
                a["rel_v"], a["gn_out"], a["wg"], a["w1"], a["b1"], a["w2"], a["b2"], a["consts"], tok_scratch,
                out.rearrange("b l c -> (b l) c"))


def shape_constants(np):
    c = np.zeros((P, NCONST), np.float32)
    p = np.arange(P)

    def put(name, value):
        a, w = CO[name]
        c[:, a:a + w] = value

    put("ident", np.eye(P))
    put("ones", 1.0 / P)
    put("g8", (p[:, None] // 8 == p[None] // 8) / 8.0)
    put("g4", (p[:, None] // 4 == p[None] // 4) / 4.0)
    put("mask_bh", p[:, None] // DK == np.arange(BH)[None])
    put("mask_r", p[:, None] // HD == np.arange(8)[None])
    put("mask_q", p[:, None] % 8 == np.arange(8)[None])
    w = np.zeros((P, 112 + HD + 112))
    w[:, 112:112 + HD] = p[:, None] % HD == np.arange(HD)[None]
    put("place", w)
    return c


def kernel(**inputs):
    import numpy as np
    import concourse.bacc as bacc
    from concourse.bass_utils import run_bass_kernel_spmd

    i = {k: np.asarray(v) for k, v in inputs.items()}
    qkv = i["L0_attn_W_qkv"].reshape(P, H, 2 * HD)
    parts = (slice(0, DK), slice(DK, 2 * DK), slice(2 * DK, 2 * HD))

    def gn_columns(v):
        q, k, val = (v.reshape(H, 2 * HD)[:, s].reshape(-1) for s in parts)
        return [np.concatenate([q, q]), np.concatenate([k, k]), val, val]

    rel = i["L0_attn_rel_emb"]
    arrays = {
        "x": i["x"], "txt": i["txt"],
        "w_tok": i["L0_tok_W"].reshape(P, ROWS, PATCH).transpose(1, 2, 0),
        "b_tok": i["L0_tok_b"].reshape(P, 1), "cls": i["L0_tok_class_token"].reshape(P, 1),
        "pos": i["L0_tok_pos_embed"].T,
        "wq": qkv[:, :, parts[0]].reshape(P, -1), "wk": qkv[:, :, parts[1]].reshape(P, -1), "wv": qkv[:, :, parts[2]].reshape(P, -1),
        "gn_in": np.stack(gn_columns(i["L0_attn_gn_qkv_scale"]) + gn_columns(i["L0_attn_gn_qkv_bias"]), 1),
        "rel_rev": rel[0:HD, ::-1], "rel_v": rel[HD:2 * HD].T[np.maximum(np.arange(LP + P)[None] - np.arange(P)[:, None] + 64, 0)].reshape(P, -1),
        "gn_out": np.stack([i["L0_attn_gn_out_scale"], i["L0_attn_gn_out_bias"]], 1),
        "wg": i["L0_ffn_Wg"], "w1": i["L0_ffn_W1"], "b1": i["L0_ffn_b1"].reshape(NF, P).T,
        "w2": i["L0_ffn_W2"].reshape(NF, P, P).transpose(1, 0, 2), "b2": i["L0_ffn_b2"].T,
        "consts": shape_constants(np),
    }
    arrays = {f"in_{k}": np.ascontiguousarray(v) for k, v in arrays.items()}
    nc = bacc.Bacc("TRN2", target_bir_lowering=False, num_devices=1)
    aps = {k[3:]: nc.dram_tensor(k, v.shape, mybir.dt.from_np(v.dtype), kind="ExternalInput").ap() for k, v in arrays.items()}
    out = nc.dram_tensor("out", (B, L, P), F32, kind="ExternalOutput").ap()
    build(nc, aps, out)
    return run_bass_kernel_spmd(nc, [arrays], core_ids=[0]).results[0]["out"]
```

```python
from contextlib import ExitStack

import concourse.bass as bass
from concourse import mybir

F32 = mybir.dt.float32
F32R = mybir.dt.float32r
BF16 = mybir.dt.bfloat16
ACT = mybir.ActivationFunctionType
ALU = mybir.AluOpType
AX = mybir.AxisListType.X

P = 128
B, C_IN, IMG = 64, 3, 224
NP_, PATCH = 8, 28
NPATCH = NP_ * NP_
ROWS = C_IN * PATCH
TXT = 128
L = 1 + NPATCH + TXT
PAIRS = B // 2
T2 = 2 * L
H, HD, DK = 8, 16, 8
BH = 2 * H
OCT = 25
LP = 8 * OCT
GRP = 4
NG = (OCT + GRP - 1) // GRP
JC = [(0, 128), (128, L - 128)]
E, FF = 8, 512
NF = E * FF // P
RING = 4
LAG = 3
SUM_LAG = 2
GT = [(0, 97), (97, 97), (194, 96), (290, 96)]
GO = [0, 97, L, L + 96]
GW = 97
LN_EPS, GN_EPS = 1e-5, 1e-4
NB0 = 4
NT0 = B // NB0
PARTS0 = 4

CO = {}
_at = 0
for _n, _w in (("ident", P), ("ones", P), ("g8", P), ("g4", P), ("mask_bh", BH), ("mask_r", 8), ("mask_q", 8),
               ("place", 112 + HD + 112)):
    CO[_n] = (_at, _w)
    _at += _w
NCONST = _at

EARLY = "txt mean1 var1 inv1 bc1 proj gmean gvar gaff glo qs0 qs1 sel0 sel1 sel2".split()
OUTPUT = "w2t ot otr ocopy".split()
SCHEDULE = (
    "c sel3 c sel4 c qs2 sel5 c sel6 c qs3 sel7 c vt0 hkeep max0 c max1 c max2 c mrow c vt1 scores c pv0 c rec0 "
    "pv1 rel place0 txt place1 c c omean mean1 c ovar c var1 oaff c inv1 oh2 c bc1 mean2 c c var2 proj c inv2 c "
    "gmean bc2 c gvar c gate c gaff c gate2 c glo top c c bcast w2t xin w2t sel0 w2t ot a sel1 qs0 otr a ocopy "
    "hres sel2 qs1 a"
).split()
AHEAD = SCHEDULE.count("a")

assert SCHEDULE.count("c") + AHEAD == NF and SCHEDULE.count("w2t") == LAG and AHEAD <= LAG


MAX_FILLS = {"max0": range(4), "max1": range(4, 8), "max2": range(8, 13)}


def is_first(t):
    return isinstance(t, int) and t == 0


def resident(nc, ctx):
    sb = lambda n, s: ctx.enter_context(nc.sbuf_tensor(n, s, F32))
    return dict(
        con=sb("con", [P, NCONST]),
        wq_z=sb("wq_z", [P, 192]),
        wk_z=sb("wk_z", [P, 192]),
        wv_s=sb("wv_s", [P, P]),
        vec=sb("vec", [P, 16]),
        pos_s=sb("pos_s", [P, 1 + NPATCH]),
        wg_s=sb("wg_s", [P, E]),
        b1_s=sb("b1_s", [P, NF]),
        b2_s=sb("b2_s", [P, E]),
        rv=sb("rv", [P, (LP + P) * HD]),
        w2_s=sb("w2_s", [P, NF, P]),
        t1=sb("t1", [P, 2 * LP]),
        const_in=ctx.enter_context(nc.semaphore("const_in")))


N_CONST = 16 * (15 + 8)


def patch_embed(nc, a, tok_scratch, R):
    with ExitStack() as ctx:
        sb = lambda n, s, d=F32: ctx.enter_context(nc.sbuf_tensor(n, s, d))
        sem = lambda n: ctx.enter_context(nc.semaphore(n))
        n = NB0 * NPATCH
        wt_hi, wt_lo = sb("wt_hi", [P, PATCH, P], F32R), sb("wt_lo", [P, PATCH, P], F32R)
        xt = sb("xt", [ROWS, 2, NB0 * NP_ * IMG])
        xh, xl = sb("xh", [P, PATCH, n], F32R), sb("xl", [P, PATCH, n], F32R)
        tok = sb("tok", [P, 2, n])
        wt = xt[:, 1, 0:PATCH * P].rearrange("p (s h) -> p s h", h=P)
        ps = [ctx.enter_context(nc.psum_tensor(f"tok_ps{i}", [P, 512], F32)) for i in range(2)]
        zeroed, w_in, w_hi_ready, w_ready = sem("zeroed"), sem("w_in"), sem("w_hi_ready"), sem("w_ready")
        tok_copied, hi_ready, lo_ready, part_used = (
            sem(n_) for n_ in "tok_copied hi_ready lo_ready part_used".split())
        x_in = [sem(f"x_in{i}") for i in range(2)]
        tok_out = [sem(f"tok_out{i}") for i in range(2)]
        block = ctx.enter_context(nc.Block())
        QS = PATCH // PARTS0

        def load(sp, i, slot):
            for b in range(NB0):
                for c in range(C_IN):
                    src = a["x"][bass.ds(i * NB0 + b, 1), c, :, :].rearrange("b (y r) w -> r (b y) w", r=PATCH)
                    dst = xt[c * PATCH:(c + 1) * PATCH, slot, b * NP_ * IMG:(b + 1) * NP_ * IMG]
                    sp.dma_start(dst.rearrange("r (y w) -> r y w", w=IMG), src).then_inc(x_in[slot], 16)

        def store(sp, i, slot):
            sp.wait_ge(tok_copied, i + 3)
            sp.dma_start(tok_scratch[:, bass.ds(i * NB0, NB0), :],
                         tok[:, slot, :].rearrange("p (b n) -> p b n", b=NB0)).then_inc(tok_out[slot], 16)

        def part_of(slot, k):
            return xt[:, slot, :].rearrange("p (n s) -> p s n", s=PATCH)[:, k * QS:(k + 1) * QS, :]

        @block.sync
        def _(sp):
            sp.dma_start(wt, a["w_tok"]).then_inc(w_in, 16)
            load(sp, 0, 0)
            sp.wait_ge(w_ready, 1)
            load(sp, 1, 1)
            with sp.Fori(0, NT0 // 2 - 1) as k:
                for slot in range(2):
                    sp.wait_ge(lo_ready, k * (2 * PARTS0) + (slot + 1) * PARTS0)
                    load(sp, k * 2 + 2 + slot, slot)
                    store(sp, k * 2 + slot, slot)
            for slot in range(2):
                store(sp, NT0 - 2 + slot, slot)
            for slot in range(2):
                sp.wait_ge(tok_out[slot], NT0 // 2 * 16 + 16)

        @block.gpsimd
        def _(pool):
            for x in (wt_hi, wt_lo):
                nc.gpsimd.memset(x[64:P, :, :].bitcast(F32), 0.0).then_inc(zeroed, 1)
            vec = R["vec"]
            for dst, src in [(R["con"][:, :], a["consts"]), (R["wq_z"][:, 64:128], a["wq"]), (R["wk_z"][:, 64:128], a["wk"]),
                             (R["wv_s"][:, :], a["wv"]), (vec[:, 0:4], a["gn_in"][:, 0:4]), (vec[:, 4:8], a["gn_in"][:, 4:8]),
                             (vec[:, 8:10], a["gn_out"]), (vec[:, 10:11], a["b_tok"]), (vec[:, 11:12], a["cls"]),
                             (R["pos_s"][:, :], a["pos"]), (R["wg_s"][:, :], a["wg"]), (R["b1_s"][:, :], a["b1"]),
                             (R["b2_s"][:, :], a["b2"]), (R["w2_s"][:, :, :], a["w2"]), (R["rv"][:, :], a["rel_v"])]:
                pool.dma_start(dst, src).then_inc(R["const_in"], 16)
            for r in range(8):
                c0 = 126 - r
                pool.dma_start(R["t1"][r:P - 7 + r:8, 0:2 * L - 1], a["rel_rev"][:, c0:c0 + 2 * L - 1]).then_inc(R["const_in"], 16)

        @block.tensor
        def _(pe):
            mm = nc.tensor.matmul
            pe.wait_ge(w_ready, 1)
            with pe.Fori(0, NT0 // 2) as k:
                for slot in range(2):
                    pe.wait_ge(tok_copied, k * 2 + slot + 1)
                    for q in range(PARTS0):
                        pe.wait_ge(lo_ready, k * (2 * PARTS0) + slot * PARTS0 + q + 1)
                        for s in range(q * QS, (q + 1) * QS):
                            o = ps[slot][:, 0:n]
                            mm(o, wt_hi[:, s, :], xh[:, s, :], start=(s == 0), stop=False)
                            mm(o, wt_hi[:, s, :], xl[:, s, :], start=False, stop=False)
                            m = mm(o, wt_lo[:, s, :], xh[:, s, :], start=False, stop=(s == PATCH - 1))
                        m.then_inc(part_used, 1)

        @block.scalar
        def _(act):
            act.wait_ge(w_in, 16)
            act.wait_ge(zeroed, 4)
            nc.scalar.activation(wt_hi[0:ROWS, :, :], wt, ACT.Copy).then_inc(w_hi_ready, 1)

            def copy_tokens(k, slot):
                act.wait_ge(part_used, k * (2 * PARTS0) + (slot + 2) * PARTS0)
                act.wait_ge(tok_out[slot], k * 16 + 16)
                nc.scalar.activation(tok[:, slot, :], ps[slot][:, 0:n], ACT.Copy).then_inc(tok_copied, 1)

            def split(k, slot, before_last):
                act.wait_ge(x_in[slot], (k + 1) * (16 * C_IN * NB0))
                for q in range(PARTS0):
                    act.wait_ge(part_used, k * (2 * PARTS0) + slot * PARTS0 + q + 1)
                    if q == PARTS0 - 1:
                        before_last()
                    nc.scalar.activation(xh[0:ROWS, q * QS:(q + 1) * QS, :], part_of(slot, q), ACT.Copy).then_inc(hi_ready, 1)

            split(0, 0, lambda: None)
            split(0, 1, lambda: copy_tokens(0, 0))
            with act.Fori(0, NT0 // 2 - 1) as k:
                split(k + 1, 0, lambda: copy_tokens(k, 1))
                split(k + 1, 1, lambda: copy_tokens(k + 1, 0))
            copy_tokens(NT0 // 2 - 1, 1)

        @block.vector
        def _(dve):
            v = nc.vector
            for x in (xh, xl):
                v.memset(x[64:P, :, :].bitcast(F32), 0.0).then_inc(zeroed, 1)
            dve.wait_ge(w_hi_ready, 1)
            v.tensor_tensor(wt_lo[0:ROWS, :, :], wt, wt_hi[0:ROWS, :, :].bitcast(F32), ALU.subtract).then_inc(w_ready, 1)
            dve.sem_inc(tok_copied, 2)
            dve.sem_inc(part_used, PARTS0)
            for slot in range(2):
                dve.sem_inc(tok_out[slot], 16)
            with dve.Fori(0, NT0 // 2) as k:
                for slot in range(2):
                    for q in range(PARTS0):
                        dve.wait_ge(hi_ready, k * (2 * PARTS0) + slot * PARTS0 + q + 1)
                        w = slice(q * QS, (q + 1) * QS)
                        v.tensor_tensor(xl[0:ROWS, w, :], part_of(slot, q), xh[0:ROWS, w, :].bitcast(F32), ALU.subtract).then_inc(lo_ready, 1)

def fused_block(nc, txt, w1, tok_scratch, out, R):
    with ExitStack() as ctx:
        sb = lambda n, s, d=F32: ctx.enter_context(nc.sbuf_tensor(n, s, d))
        sem = lambda n: ctx.enter_context(nc.semaphore(n))

        con, wq_z, wk_z, wv_s, vec, pos_s, wg_s, b1_s, b2_s, rv, w2_s, t1 = (
            R[n] for n in "con wq_z wk_z wv_s vec pos_s wg_s b1_s b2_s rv w2_s t1".split())
        K = {n: con[:, a:a + w] for n, (a, w) in CO.items()}
        ident, ones, g8, g4 = K["ident"], K["ones"], K["g8"], K["g4"]
        pick_o = sb("pick_o", [64, 32], BF16)
        sel_z = sb("sel_z", [P, 64 + BH * P], F32R)
        b2x2 = sb("b2x2", [P, 1])
        half = sb("half", [P, 2])
        rw_hi = sb("rw_hi", [P, 2 * L], F32R)
        rw_lo = sb("rw_lo", [P, 2 * L], F32R)
        w1_hi = sb("w1_hi", [P, NF * P], F32R)
        w1_lo = sb("w1_lo", [P, NF * P], F32R)

        tok = sb("tok2", [P, 2, NPATCH])
        txt_s = sb("txt_s", [P, 2, P])
        h = sb("h", [P, 2, L])
        h2 = sb("h2", [P, T2])
        t2 = sb("t2", [P, 2 * LP])
        e1 = sb("e1", [P, 2 * LP])
        e2 = sb("e2", [P, 2 * LP])
        q_f, k_f = sb("q_f", [P, 2 * LP], F32R), sb("k_f", [P, 2 * LP], F32R)
        (q_hi, q_lo), (k_hi, k_lo) = ((x[:, 0:LP], x[:, LP:2 * LP]) for x in (q_f, k_f))
        st, st_o = sb("st", [P, 4, 6]), sb("st_o", [P, 2, 6])
        mv, mv_o = sb("mv", [P, 4, 2]), sb("mv_o", [P, 2, 2])
        gst, gst_o = (sb(n, [P, 7, 4]) for n in ("gst", "gst_o"))
        q_bd = [sb(f"q_bd_{n}", [P, OCT, BH, 8], F32R) for n in ("hi", "lo")]
        a_f = sb("a_f", [P, 2, OCT, BH, 8], F32R)
        a_bd = [a_f[:, z, :, :, :] for z in range(2)]
        mx = sb("mx", [P, 32])
        mt = sb("mt", [64, P], BF16)
        pr = [sb(f"probs{c}", [P, OCT, BH, 8]) for c in range(2)]
        v_pad = sb("v_pad", [P, 2, H, P])
        top8 = sb("top8", [P, 4, 8])
        dl = sb("dl", [P, 8])
        wait_slot = sb("wait_slot", [P, 4])
        ep = sb("ep", [P, 8])
        ep_t = sb("ep_t", [8, GW])
        rs1, rs2 = sb("rs1", [P, 4]), sb("rs2", [P, 4])
        rs1_t, rs2_t = sb("rs1_t", [4, GW]), sb("rs2_t", [4, GW])
        x_hi = sb("x_hi", [P, T2], F32R)
        x_lo = sb("x_lo", [P, T2], F32R)
        ratio = sb("ratio", [P, T2])
        hres = sb("hres", [P, T2])
        gelu1 = sb("gelu1", [P, RING, T2])
        gelu2 = sb("gelu2", [P, RING, T2])
        o_s = sb("o_s", [P, 4, P])
        w1_st = [x[:, :, :, :].rearrange("p a b c -> p (a b c)")[:, 0:4 * FF] for x in pr]

        bank = [ctx.enter_context(nc.psum_tensor(f"bank{i}", [P, 512], F32)) for i in range(8)]
        zb, yb, lg, pv, misc = bank[0:2], bank[2], bank[3:5], bank[5:7], bank[7]
        LN = {"1": (misc, e1, e2, rs1, rs1_t), "2": (pv[0], t1, t2, rs2, rs2_t)}

        names = """w1_in w1_hi_ready w1_split setup_dve setup_pool setup_act tok_in txt_t h_ready qk_ready v_ready
            bn mv_ready gmean gspread gvar gve grstd affine_part affine norm lo q_spread sel_done max_done mx_t mt_ready
            vt v_copied exp_done wm_done pv_done pv_ready rec_done o_part obn omv omean ospread ovar ove orstd oaff_part oaffine
            onorm h2_ready logits top_done dl_ready e_ready e1_ready p1_ready ep_tr ep_copied bcast_ready
            xp_done ffn_in xh_done gtmp otmp mt_hi sel_ready max_ready scores rel_ready z_ready z2_done g_done hres_done h_kept hs_done w2_done ot_ready o_t os_ready out_done""".split()
        S = {n: sem(n) for n in names}
        S["const_in"] = R["const_in"]
        for k in ("1", "2"):
            for n in ("mean", "delta", "square", "var", "vareps", "rstd", "rstd_tr", "rstd_row", "rstd_bc", "x"):
                S[n + k] = sem(n + k)

        GS, GB, OS, OB, BT, CL = vec[:, 0:4], vec[:, 4:8], vec[:, 8:9], vec[:, 9:10], vec[:, 10:11], vec[:, 11:12]
        V2 = lambda t: t[:, 0:T2]
        block = ctx.enter_context(nc.Block())

        def turn(attend, mlp, end, n, late, early):
            f, ahead, w = AHEAD, 0, NF - LAG
            for s in SCHEDULE:
                if s == "c":
                    if n is not None:
                        mlp(f, n)
                    f += 1
                elif s == "a":
                    if late is not None:
                        mlp(ahead, late)
                    ahead += 1
                elif s in OUTPUT:
                    if n is not None:
                        end(s, n, w)
                    w += s == "w2t"
                elif s in EARLY:
                    if early is not None:
                        attend(s, early)
                elif late is not None:
                    attend(s, late)

        def turns(eng, attend, mlp, end, setup=lambda: None):
            for s in EARLY:
                attend(s, 0)
            setup()
            turn(attend, mlp, end, None, 0, 1)
            with eng.Fori(0, PAIRS - 2) as n:
                turn(attend, mlp, end, n, n + 1, n + 2)
            turn(attend, mlp, end, PAIRS - 2, PAIRS - 1, None)
            turn(attend, mlp, end, PAIRS - 1, None, None)

        def ring_wait(eng, sem_, f, n):
            if f >= RING or not is_first(n):
                eng.wait_ge(sem_, n * NF + f - RING + 1)

        @block.sync
        def _(sp):
            def tokens(t):
                sp.dma_start(tok[:, :, :], tok_scratch[:, bass.ds(t * 2, 2), :]).then_inc(S["tok_in"], 16)
                sp.dma_start(txt_s[:, :, :], txt[bass.ds(t * 2, 2), :, :].rearrange("b t c -> t b c")).then_inc(S["tok_in"], 16)

            def store(n):
                sp.wait_ge(S["os_ready"], n * 2 + 4)
                for k, (a, w) in enumerate(GT):
                    sp.dma_start(out[bass.ds(n * T2 + a, w), :], o_s[0:w, k, :]).then_inc(S["out_done"], 16)

            tokens(0)
            for piece in range(2):
                sp.dma_start(w1_st[piece].rearrange("d (e f) -> d e f", f=FF),
                             w1[4 * piece:4 * piece + 4, :, :].rearrange("e d f -> d e f")).then_inc(S["w1_in"], 16)
            for t in range(2):
                sp.wait_ge(S["h_ready"], t * 2 + 2)
                tokens(t + 1)
            with sp.Fori(0, PAIRS - 3) as n:
                sp.wait_ge(S["h_ready"], n * 2 + 6)
                tokens(n + 3)
                store(n)
            store(PAIRS - 3)
            store(PAIRS - 2)
            store(PAIRS - 1)
            sp.wait_ge(S["out_done"], 64 * PAIRS + 64)

        @block.tensor
        def _(pe):
            mm = nc.tensor.matmul

            def w2_step(f, n):
                if f == 0:
                    pe.wait_ge(S["os_ready"], n * 2 + 2)
                pe.wait_ge(S["hs_done"], n * NF + f + 1)
                mm(yb[:, 0:T2], w2_s[:, f, :], gelu1[:, f % RING, :], start=(f == 0), stop=(f == NF - 1)).then_inc(S["w2_done"], 1)

            def mlp(f, n):
                if f == 0:
                    pe.wait_ge(S["xh_done"], n + 1)
                if f >= 2 or not is_first(n):
                    pe.wait_ge(S["g_done"], n * (2 * NF) + 2 * (f - 2) + 1)
                z = zb[f % 2][:, 0:T2]
                w = slice(f * P, (f + 1) * P)
                mm(z, w1_hi[:, w], x_hi[:, :], start=True, stop=False)
                mm(z, w1_lo[:, w], x_hi[:, :], start=False, stop=False)
                if f == 0:
                    pe.wait_ge(S["ffn_in"], n * 2 + 2)
                mm(z, w1_hi[:, w], x_lo[:, :], start=False, stop=True).then_inc(S["z_ready"], 1)
                if f >= LAG:
                    w2_step(f - LAG, n)

            def end(s, n, f):
                if s == "w2t":
                    w2_step(f, n)
                elif s == "otr":
                    pe.wait_ge(S["ot_ready"], n + 1)
                    for k, (a, w) in enumerate(GT):
                        i = nc.tensor.transpose(yb[0:w, k * P:(k + 1) * P], hres[:, a:a + w], ident)
                    i.then_inc(S["o_t"], 1)

            def mean_of(k, t):
                pe.wait_ge(S["h_ready" if k == "1" else "h2_ready"], t * 2 + 2)
                src = h[:, :, :].rearrange("p b l -> p (b l)") if k == "1" else h2[:, :]
                mm(LN[k][0][:, 0:T2], ones, src, start=True, stop=True).then_inc(S["mean" + k], 1)

            def var_of(k, t):
                ps, _, sq, _, _ = LN[k]
                pe.wait_ge(S["square" + k], t + 1)
                for i, a in enumerate(GO):
                    m = mm(ps[0:GW, i:i + 1], sq[:, a:a + GW], ones[:, 0:1], start=True, stop=True)
                m.then_inc(S["var" + k], 1)

            def broadcast(ps, rows, first, src):
                for i, a in enumerate(GO):
                    m = mm(ps[:, a:a + GW], ident[0:rows, first + i:first + i + 1].broadcast_to([rows, P]), src,
                           start=True, stop=True)
                return m

            def transpose_v(b, t):
                if b == 0:
                    pe.wait_ge(S["norm"], t * 6 + 6)
                for c, (j0, jn) in enumerate(JC):
                    i = nc.tensor.transpose(misc[0:jn, c * P:(c + 1) * P], e2[:, b * L + j0:b * L + j0 + jn], ident)
                i.then_inc(S["vt"], 1)

            def attend(s, t):
                if s == "txt":
                    pe.wait_ge(S["tok_in"], t * 32 + 32)
                    if not is_first(t):
                        pe.wait_ge(S["v_copied"], t * 4)
                    for b in range(2):
                        i = nc.tensor.transpose(misc[:, b * P:(b + 1) * P], txt_s[:, b, :], ident)
                    i.then_inc(S["txt_t"], 1)
                elif s in ("mean1", "mean2"):
                    mean_of(s[4], t)
                elif s in ("var1", "var2"):
                    var_of(s[3], t)
                elif s in ("inv1", "inv2"):
                    pe.wait_ge(S["rstd" + s[3]], t + 1)
                    ps, _, _, rs, _ = LN[s[3]]
                    nc.tensor.transpose(ps[0:4, 0:GW], rs[0:GW, 0:4], ident[0:GW, 0:GW]).then_inc(S["rstd_tr" + s[3]], 1)
                elif s in ("bc1", "bc2"):
                    pe.wait_ge(S["rstd_row" + s[2]], t + 1)
                    ps, _, _, _, rs_t = LN[s[2]]
                    broadcast(ps, 4, 0, rs_t[:, :]).then_inc(S["rstd_bc" + s[2]], 1)
                elif s == "proj":
                    pe.wait_ge(S["x1"], t + 1)
                    for wz, c0 in ((wq_z, 0), (wk_z, 256)):
                        for b in range(2):
                            i = mm(misc[:, c0:c0 + L], wz[:, 64 - 64 * b:192 - 64 * b], e2[:, b * L:(b + 1) * L],
                                   start=(b == 0), stop=(b == 1))
                    i.then_inc(S["qk_ready"], 1)
                    mm(lg[0][:, 0:T2], wv_s[:, :], V2(e2), start=True, stop=True).then_inc(S["v_ready"], 1)
                elif s == "gmean":
                    pe.wait_ge(S["mv_ready"], t * 4 + 4)
                    mm(lg[1][:, 0:4], g8, mv[:, :, 0], start=True, stop=True).then_inc(S["gmean"], 1)
                elif s == "gvar":
                    pe.wait_ge(S["gspread"], t + 1)
                    mm(lg[1][:, 0:4], g8, gst[:, 3, :], start=True, stop=True).then_inc(S["gvar"], 1)
                elif s[:3] == "sel":
                    part = int(s[3])
                    if part == 0:
                        pe.wait_ge(S["norm"], t * 6 + 6)
                        pe.wait_ge(S["lo"], t * 2 + 2)
                    for bh in range(2 * part, 2 * part + 2):
                        if bh >= 2:
                            pe.wait_ge(S["sel_done"], t * BH + bh - 1)
                        for z, x in ((0, k_f), (1, q_f)):
                            c0 = 64 - 64 * z + P * bh
                            m = mm(lg[bh % 2][:, 0:2 * LP], sel_z[:, c0:c0 + P], x[:, :], start=(z == 0), stop=(z == 1))
                        m.then_inc(S["sel_ready"], 1)
                elif s == "vt0":
                    transpose_v(0, t)
                elif s[:3] == "max":
                    if s == "max0":
                        pe.wait_ge(S["q_spread"], t * 4 + 2)
                    for i in MAX_FILLS[s]:
                        pe.wait_ge(S["sel_done"], t * BH + BH) if i < 2 else pe.wait_ge(S["max_done"], t * 13 + i - 1)
                        for k in range(2 if 2 * i + 1 < OCT else 1):
                            o = 2 * i + k
                            dst = lg[i % 2][:, k * 256:k * 256 + L + 1]
                            mm(dst, q_bd[0][:, o, :, :], k_hi[:, 0:L + 1], start=True, stop=False)
                            m = mm(dst, a_bd[0][:, o, :, :], rw_hi[:, 192 - 8 * o:192 - 8 * o + L + 1], start=False, stop=True)
                        m.then_inc(S["max_ready"], 1)
                elif s == "mrow":
                    pe.wait_ge(S["max_done"], t * 13 + 13)
                    pe.wait_ge(S["v_copied"], t * 4 + 2)
                    nc.tensor.transpose(misc[0:OCT, 0:P], mx[:, 0:OCT], ident).then_inc(S["mx_t"], 1)
                elif s == "vt1":
                    pe.wait_ge(S["mt_ready"], t + 1)
                    transpose_v(1, t)
                elif s == "scores":
                    pe.wait_ge(S["q_spread"], t * 4 + 4)
                    i = 0
                    for g in range(NG):
                        octs = range(g * GRP, min(OCT, (g + 1) * GRP))
                        for c, (j0, jn) in enumerate(JC):
                            pe.wait_ge(S["max_done"], t * 13 + 12 + i) if i < 2 else pe.wait_ge(S["exp_done"], t * 14 + i - 1)
                            ps = lg[(1 + i) % 2]
                            whole = ps[0:jn, 0:len(octs) * P]
                            js = slice(j0, j0 + jn)
                            os_ = slice(octs[0], octs[-1] + 1)
                            mm(whole, k_hi[:, js], q_bd[0][:, os_, :, :], start=True, stop=False)
                            mm(whole, k_lo[:, js], q_bd[0][:, os_, :, :], start=False, stop=False)
                            mm(whole, k_hi[:, js], q_bd[1][:, os_, :, :], start=False, stop=False)
                            for o in octs:
                                part = ps[0:jn, (o - octs[0]) * P:(o - octs[0] + 1) * P]
                                win = slice(192 - 8 * o + j0, 192 - 8 * o + j0 + jn)
                                mm(part, rw_hi[:, win], a_bd[0][:, o, :, :], start=False, stop=False)
                                mm(part, rw_lo[:, win], a_bd[0][:, o, :, :], start=False, stop=False)
                                mm(part, rw_hi[:, win], a_bd[1][:, o, :, :], start=False, stop=False)
                                m = mm(part, pick_o[0:32 + OCT, o:o + 1].broadcast_to([32 + OCT, jn]), mt[0:32 + OCT, :],
                                       start=False, stop=(o == octs[-1]))
                            m.then_inc(S["scores"], 1)
                            i += 1
                elif s in ("pv0", "pv1"):
                    b = int(s[2])
                    pe.wait_ge(S["exp_done"], t * 14 + 14)
                    pe.wait_ge(S["v_copied"], t * 4 + 2 + 2 * b)
                    for hh in range(H):
                        for c, (j0, jn) in enumerate(JC):
                            m = mm(pv[b][:, hh // 4 * 256:hh // 4 * 256 + LP], v_pad[0:jn, c, hh, :],
                                   pr[c][0:jn, :, H * b + hh, :], start=(hh == 0 and c == 0), stop=False,
                                   skip_group_check=True)
                    m.then_inc(S["pv_done"], 1)
                elif s == "rel":
                    for g in range(NG):
                        octs = range(g * GRP, min(OCT, (g + 1) * GRP))
                        if g >= 2:
                            pe.wait_ge(S["wm_done"], t * NG + g - 1)
                        ps = lg[(1 + g) % 2]
                        for o in octs:
                            part = ps[:, (o - octs[0]) * P:(o - octs[0] + 1) * P]
                            mm(part, rv[:, (8 * o + P) * HD:(8 * o + P) * HD + P], pr[0][:, o, :, :], start=True, stop=False)
                            m = mm(part, rv[0:JC[1][1], 8 * o * HD:8 * o * HD + P], pr[1][0:JC[1][1], o, :, :],
                                   start=False, stop=True)
                        m.then_inc(S["rel_ready"], 1)
                elif s in ("place0", "place1"):
                    b = int(s[5])
                    pe.wait_ge(S["wm_done"], t * NG + NG)
                    pe.wait_ge(S["rec_done"], t * 4 + 2 * b + 2)
                    for hh in range(H):
                        m = mm(pv[b][:, hh // 4 * 256:hh // 4 * 256 + LP], K["place"][:, 112 - 16 * hh:112 - 16 * hh + P],
                               pr[0][:, :, H * b + hh, :], start=False, stop=(hh == H - 1), skip_group_check=True)
                    m.then_inc(S["pv_ready"], 1)
                elif s == "omean":
                    pe.wait_ge(S["omv"], t * 2 + 2)
                    mm(pv[0][:, 0:2], g4, mv_o[:, :, 0], start=True, stop=True).then_inc(S["omean"], 1)
                elif s == "ovar":
                    pe.wait_ge(S["ospread"], t + 1)
                    mm(pv[0][:, 0:2], g4, gst_o[:, 3, 0:2], start=True, stop=True).then_inc(S["ovar"], 1)
                elif s == "gate":
                    pe.wait_ge(S["x2"], t + 1)
                    for k, a in enumerate(GO):
                        m = mm(pv[0][0:GW, 8 * k:8 * k + 8], t2[:, a:a + GW], wg_s[:, :], start=True, stop=True)
                    m.then_inc(S["logits"], 1)
                elif s == "top":
                    pe.wait_ge(S["p1_ready"], t + 1)
                    nc.tensor.transpose(pv[0][0:8, 0:GW], ep[0:GW, :], ident[0:GW, 0:GW]).then_inc(S["ep_tr"], 1)
                elif s == "bcast":
                    pe.wait_ge(S["ep_copied"], t + 1)
                    broadcast(pv[0], 8, 0, ep_t[:, :])
                    broadcast(pv[1], 8, 4, ep_t[:, :]).then_inc(S["bcast_ready"], 1)

            pe.wait_ge(S["const_in"], N_CONST)
            pe.wait_ge(S["setup_dve"], 15)
            turns(pe, attend, mlp, end, lambda: pe.wait_ge(S["w1_split"], 2))

        @block.vector
        def _(dve):
            v = nc.vector

            def carry_wait(k):
                v.memset(wait_slot[:, k:k + 1], 0.0)

            def mlp(f, n):
                dve.wait_ge(S["z_ready"], n * NF + f + 1)
                ring_wait(dve, S["hs_done"], f, n)
                v.tensor_tensor(gelu2[:, f % RING, :], zb[f % 2][:, 0:T2], ratio[:, :], ALU.mult).then_inc(S["z2_done"], 1)

            def end(s, n, _f):
                if s == "ot":
                    dve.wait_ge(S["w2_done"], n * NF + NF)
                    dve.wait_ge(S["hres_done"], n + 1)
                    v.tensor_tensor(hres[:, :], yb[:, 0:T2], hres[:, :], ALU.add).then_inc(S["ot_ready"], 1)
                elif s == "ocopy":
                    dve.wait_ge(S["o_t"], n + 1)
                    dve.wait_ge(S["out_done"], n * 64 + 64)
                    v.tensor_copy(o_s[0:GW, 0:2, :], yb[0:GW, 0:2 * P].rearrange("p (k c) -> p k c", k=2)).then_inc(S["os_ready"], 1)
                    v.tensor_copy(o_s[0:96, 2:4, :], yb[0:96, 2 * P:4 * P].rearrange("p (k c) -> p k c", k=2)).then_inc(S["os_ready"], 1)

            def layernorm(s, k, t):
                src = h[:, :, :].rearrange("p b l -> p (b l)") if k == "1" else h2[:, :]
                ps, delta, sq, rs, rs_t = LN[k]
                if s == "mean":
                    dve.wait_ge(S["mean" + k], t + 1)
                    v.tensor_tensor(V2(delta), src, ps[:, 0:T2], ALU.subtract).then_inc(S["delta" + k], 1)
                    dve.wait_ge(S["delta" + k], t + 1)
                    v.tensor_tensor(V2(sq), V2(delta), V2(delta), ALU.mult).then_inc(S["square" + k], 1)
                elif s == "var":
                    dve.wait_ge(S["var" + k], t + 1)
                    v.tensor_scalar(rs[0:GW, 0:4], ps[0:GW, 0:4], LN_EPS, None, ALU.add).then_inc(S["vareps" + k], 1)
                elif s == "inv":
                    dve.wait_ge(S["rstd_tr" + k], t + 1)
                    v.tensor_copy(rs_t[:, :], ps[0:4, 0:GW]).then_inc(S["rstd_row" + k], 1)
                else:
                    dve.wait_ge(S["rstd_bc" + k], t + 1)
                    v.tensor_tensor(V2(sq), V2(delta), ps[:, 0:T2], ALU.mult).then_inc(S["x" + k], 1)

            def group_spread(m, stats, gs, psum, ready, tmp, done, t):
                gm, dm, d2, spread = (gs[:, i, 0:m] for i in range(4))
                dve.wait_ge(ready, t + 1)
                v.tensor_copy(gm, psum)
                v.tensor_tensor(dm, stats[:, 0:m, 0], psum, ALU.subtract).then_inc(tmp, 1)
                dve.wait_ge(tmp, t * 2 + 1)
                v.tensor_tensor(d2, dm, dm, ALU.mult).then_inc(tmp, 1)
                dve.wait_ge(tmp, t * 2 + 2)
                v.tensor_tensor(spread, d2, stats[:, 0:m, 1], ALU.add).then_inc(done, 1)

            def group_affine(m, gs, rstd, part, done, scale, bias, t):
                gm, _, d2, _, rs, sc, bi = (gs[:, i, 0:m] for i in range(7))
                dve.wait_ge(rstd, t + 1)
                v.tensor_tensor(sc, scale, rs, ALU.mult).then_inc(part, 1)
                dve.wait_ge(part, t * 2 + 1)
                v.tensor_tensor(d2, gm, sc, ALU.mult).then_inc(part, 1)
                dve.wait_ge(part, t * 2 + 2)
                v.tensor_tensor(bi, bias, d2, ALU.subtract).then_inc(done, 1)

            HALVES = ((0, 0, 64), (256, 64, 0))

            def reciprocal(b, part, t):
                dve.wait_ge(S["pv_done"], t * 2 + b + 1)
                a, n_, d_ = HALVES[part]
                v.reciprocal(t2[n_:n_ + 64, b * L:(b + 1) * L], pv[b][d_:d_ + 64, a:a + L]).then_inc(S["rec_done"], 1)

            def attend(s, t):
                if s == "txt":
                    dve.wait_ge(S["tok_in"], t * 32 + 32)
                    if not is_first(t):
                        dve.wait_ge(S["h_kept"], t)
                    v.scalar_tensor_tensor(out=h[:, :, 1:1 + NPATCH], in0=tok[:, :, :], scalar=BT,
                                           in1=pos_s[:, 1:].unsqueeze(1).broadcast_to([P, 2, NPATCH]),
                                           op0=ALU.add, op1=ALU.mult).then_inc(S["h_ready"], 1)
                    dve.wait_ge(S["txt_t"], t + 1)
                    v.tensor_copy(h[:, :, 1 + NPATCH:], misc[:, 0:2 * P].rearrange("p (b l) -> p b l", b=2)).then_inc(S["h_ready"], 1)
                elif s in ("mean1", "mean2"):
                    layernorm("mean", s[4], t)
                elif s in ("var1", "var2"):
                    layernorm("var", s[3], t)
                elif s in ("inv1", "inv2"):
                    layernorm("inv", s[3], t)
                elif s in ("bc1", "bc2"):
                    layernorm("bc", s[2], t)
                elif s == "proj":
                    dve.wait_ge(S["qk_ready"], t + 1)
                    v.bn_stats(st[:, 0, :], misc[:, 0:L]).then_inc(S["bn"], 1)
                    v.bn_stats(st[:, 1, :], misc[:, 256:256 + L]).then_inc(S["bn"], 1)
                    dve.wait_ge(S["v_ready"], t + 1)
                    for b in range(2):
                        v.bn_stats(st[:, 2 + b, :], lg[0][:, b * L:(b + 1) * L]).then_inc(S["bn"], 1)
                    dve.wait_ge(S["bn"], t * 4 + 4)
                    carry_wait(0)
                    for k in range(4):
                        v.bn_aggr(mv[:, k, :], st[:, k, :]).then_inc(S["mv_ready"], 1)
                elif s == "gmean":
                    group_spread(4, mv, gst, lg[1][:, 0:4], S["gmean"], S["gtmp"], S["gspread"], t)
                elif s == "gvar":
                    dve.wait_ge(S["gvar"], t + 1)
                    v.tensor_scalar(gst[:, 4, :], lg[1][:, 0:4], GN_EPS, None, ALU.add).then_inc(S["gve"], 1)
                elif s == "gaff":
                    group_affine(4, gst, S["grstd"], S["affine_part"], S["affine"], GS, GB, t)
                elif s == "glo":
                    dve.wait_ge(S["norm"], t * 6 + 4)
                    for x, lo, hi in ((e1[:, 0:L], q_lo, q_hi), (e1[:, LP:LP + L], k_lo, k_hi)):
                        v.tensor_tensor(lo[:, 0:L], x, hi[:, 0:L].bitcast(F32), ALU.subtract).then_inc(S["lo"], 1)
                elif s[:3] == "sel":
                    part = int(s[3])
                    for bh in range(2 * part, 2 * part + 2):
                        dve.wait_ge(S["sel_ready"], t * BH + bh + 1)
                        v.tensor_tensor(a_f[:, :, :, bh, :],
                                        lg[bh % 2][:, 0:2 * LP].rearrange("p (z o r) -> p z o r", z=2, r=8),
                                        K["mask_q"].unsqueeze(1).unsqueeze(1).broadcast_to([P, 2, OCT, 8]),
                                        ALU.mult).then_inc(S["sel_done"], 1)
                elif s[:3] == "max":
                    for i in MAX_FILLS[s]:
                        dve.wait_ge(S["max_ready"], t * 13 + i + 1)
                        w = 2 if 2 * i + 1 < OCT else 1
                        v.tensor_reduce(mx[:, 2 * i:2 * i + w], lg[i % 2][:, :].rearrange("p (k x) -> p k x", k=2)[:, 0:w, 0:L],
                                        AX, ALU.max).then_inc(S["max_done"], 1)
                elif s == "mrow":
                    dve.wait_ge(S["mx_t"], t + 1)
                    v.tensor_scalar(mt[0:OCT, :], misc[0:OCT, 0:P], -1.0, None, ALU.mult).then_inc(S["mt_hi"], 1)
                    dve.wait_ge(S["mt_hi"], t + 1)
                    v.scalar_tensor_tensor(out=mt[32:32 + OCT, :], in0=misc[0:OCT, 0:P], scalar=-1.0, in1=mt[0:OCT, :],
                                           op0=ALU.mult, op1=ALU.subtract).then_inc(S["mt_ready"], 1)
                elif s == "rec0":
                    for half_ in range(2):
                        reciprocal(0, half_, t)
                elif s == "rel":
                    for g in range(NG):
                        w = min(OCT, (g + 1) * GRP) - g * GRP
                        if g in (2, 4):
                            reciprocal(1, g // 2 - 1, t)
                        dve.wait_ge(S["rel_ready"], t * NG + g + 1)
                        v.tensor_tensor(pr[0][:, g * GRP:g * GRP + w, :, :].rearrange("p o b r -> p (o b) r"),
                                        lg[(1 + g) % 2][:, 0:w * P].rearrange("p (x r) -> p x r", r=8),
                                        K["mask_r"].unsqueeze(1).broadcast_to([P, w * BH, 8]), ALU.mult).then_inc(S["wm_done"], 1)
                elif s in ("place0", "place1"):
                    b = int(s[5])
                    bs = slice(b * L, (b + 1) * L)
                    dve.wait_ge(S["pv_ready"], t * 2 + b + 1)
                    for k, (a, n_, _) in enumerate(HALVES):
                        dve.wait_ge(S["rec_done"], t * 4 + 2 * b + k + 1)
                        v.tensor_tensor(t1[n_:n_ + 64, bs], pv[b][n_:n_ + 64, a:a + L], t2[n_:n_ + 64, bs],
                                        ALU.mult).then_inc(S["o_part"], 1)
                    dve.wait_ge(S["o_part"], t * 4 + 2 * b + 2)
                    v.bn_stats(st_o[:, b, :], t1[:, bs]).then_inc(S["obn"], 1)
                    dve.wait_ge(S["obn"], t * 2 + b + 1)
                    carry_wait(1 + b)
                    v.bn_aggr(mv_o[:, b, :], st_o[:, b, :]).then_inc(S["omv"], 1)
                elif s == "omean":
                    group_spread(2, mv_o, gst_o, pv[0][:, 0:2], S["omean"], S["otmp"], S["ospread"], t)
                elif s == "ovar":
                    dve.wait_ge(S["ovar"], t + 1)
                    v.tensor_scalar(gst_o[:, 4, 0:2], pv[0][:, 0:2], GN_EPS, None, ALU.add).then_inc(S["ove"], 1)
                elif s == "oaff":
                    group_affine(2, gst_o, S["orstd"], S["oaff_part"], S["oaffine"],
                                 OS.broadcast_to([P, 2]), OB.broadcast_to([P, 2]), t)
                elif s == "oh2":
                    for b in range(2):
                        dve.wait_ge(S["onorm"], t * 2 + b + 1)
                        bs = slice(b * L, (b + 1) * L)
                        v.tensor_tensor(h2[:, bs], h2[:, bs], t2[:, bs], ALU.add).then_inc(S["h2_ready"], 1)
                elif s == "gate":
                    dve.wait_ge(S["logits"], t + 1)
                    carry_wait(3)
                    for k in range(4):
                        v.max(top8[0:GW, k, :], pv[0][0:GW, 8 * k:8 * k + 8]).then_inc(S["top_done"], 1)
                    dve.wait_ge(S["top_done"], t * 4 + 4)
                    v.tensor_tensor(dl[0:GW, 0:4], top8[0:GW, :, 1], top8[0:GW, :, 0], ALU.subtract).then_inc(S["dl_ready"], 1)
                elif s == "gate2":
                    dve.wait_ge(S["e_ready"], t + 1)
                    v.tensor_scalar(dl[0:GW, 4:8], ep[0:GW, 0:4], 1.0, None, ALU.add).then_inc(S["e1_ready"], 1)
                    dve.wait_ge(S["e1_ready"], t + 1)
                    v.reciprocal(ep[0:GW, 4:8], dl[0:GW, 4:8]).then_inc(S["p1_ready"], 1)
                elif s == "top":
                    dve.wait_ge(S["ep_tr"], t + 1)
                    v.tensor_copy(ep_t[:, 0:GW], pv[0][0:8, 0:GW]).then_inc(S["ep_copied"], 1)
                elif s == "bcast":
                    dve.wait_ge(S["bcast_ready"], t + 1)
                    v.tensor_tensor(V2(t1), V2(t2), pv[1][:, 0:T2], ALU.mult).then_inc(S["xp_done"], 1)
                elif s == "xin":
                    if not is_first(t):
                        dve.wait_ge(S["z2_done"], t * NF)
                    v.tensor_copy(ratio[:, :], pv[0][:, 0:T2]).then_inc(S["ffn_in"], 1)
                    dve.wait_ge(S["xh_done"], t + 1)
                    v.tensor_tensor(x_lo[:, :], V2(t1), x_hi[:, :].bitcast(F32), ALU.subtract).then_inc(S["ffn_in"], 1)
                elif s == "hres":
                    if not is_first(t):
                        dve.wait_ge(S["o_t"], t)
                    v.tensor_scalar(hres[:, :], h2[:, :], b2x2[:, :], None, ALU.add).then_inc(S["hres_done"], 1)

            z = S["setup_dve"]
            v.memset(wq_z[:, 0:64], 0.0); v.memset(wq_z[:, 128:192], 0.0)
            v.memset(wk_z[:, 0:64], 0.0); v.memset(wk_z[:, 128:192], 0.0)
            v.memset(mt[:, :], 0.0)
            for x in (q_hi, q_lo, k_hi, k_lo):
                v.memset(x[:, :].bitcast(F32), 0.0).then_inc(z, 1)
            v.memset(half[:, 0:1], -0.5).then_inc(z, 1)
            v.memset(half[:, 1:2], 2.718281828459045).then_inc(z, 1)
            v.memset(v_pad[:, :, :, :], 0.0).then_inc(z, 1)
            v.memset(sel_z[:, :].bitcast(F32), 0.0).then_inc(z, 1)
            dve.wait_ge(z, 8)
            for hh in range(H):
                c0 = (64 if hh < 4 else 0) + (hh % 4) * HD
                last = v.memset(v_pad[:, :, hh, c0:c0 + HD], 1.0)
            last.then_inc(z, 1)
            dve.wait_ge(S["const_in"], N_CONST)
            v.memset(t1[:, 2 * L - 1:2 * L], 0.0).then_inc(z, 1)
            v.tensor_copy(pick_o[0:32, :], con[0:32, 0:32])
            v.tensor_copy(pick_o[32:64, :], con[0:32, 0:32])
            v.tensor_tensor(sel_z[:, 64:].rearrange("p (b z e r) -> p b z e r", b=BH, z=2, e=8)[:, :, 0, :, :],
                            K["mask_bh"].unsqueeze(2).unsqueeze(3).broadcast_to([P, BH, 8, 8]),
                            K["mask_q"].unsqueeze(1).unsqueeze(3).broadcast_to([P, BH, 8, 8]), ALU.mult)
            for b in range(2):
                v.tensor_tensor(h[:, b, 0:1], CL, pos_s[:, 0:1], ALU.mult)
            v.tensor_reduce(b2x2[:, :], b2_s[:, :], AX, ALU.add).then_inc(z, 1)
            dve.wait_ge(z, 11)
            v.tensor_scalar(b2x2[:, :], b2x2[:, :], 2.0, None, ALU.mult).then_inc(z, 1)
            v.tensor_copy(rw_hi[:, :], V2(t1)).then_inc(z, 1)
            dve.wait_ge(z, 13)
            v.tensor_tensor(rw_lo[:, :], V2(t1), rw_hi[:, :].bitcast(F32), ALU.subtract).then_inc(z, 2)
            dve.sem_inc(S["out_done"], 64)
            dve.sem_inc(S["os_ready"], 2)

            def split_w1():
                for piece in range(2):
                    dve.wait_ge(S["w1_hi_ready"], piece + 1)
                    a = slice(2048 * piece, 2048 * piece + 2048)
                    v.tensor_tensor(w1_lo[:, a], w1_st[piece], w1_hi[:, a].bitcast(F32), ALU.subtract).then_inc(S["w1_split"], 1)

            turns(dve, attend, mlp, end, split_w1)

        @block.scalar
        def _(act):
            a = nc.scalar.activation

            def mlp(f, n):
                act.wait_ge(S["z2_done"], n * NF + f + 1)
                ring_wait(act, S["w2_done"], f, n)
                a(gelu1[:, f % RING, :], zb[f % 2][:, 0:T2], ACT.Gelu, bias=b1_s[:, f:f + 1]).then_inc(S["g_done"], 1)
                a(gelu2[:, f % RING, :], gelu2[:, f % RING, :], ACT.Gelu, bias=b1_s[:, f:f + 1]).then_inc(S["g_done"], 1)

            def copy_v(b, t):
                act.wait_ge(S["vt"], t * 2 + b + 1)
                if b == 1:
                    act.wait_ge(S["pv_done"], t * 2 + 1)
                for c, (j0, jn) in enumerate(JC):
                    blk = v_pad[0:jn, c, :, :].rearrange("p h n -> p (h n)")
                    dst = bass.AP(tensor=blk.tensor, offset=blk.offset, ap=[list(blk.ap[0]), [P + HD, H], [1, HD]])
                    a(dst, misc[0:jn, c * P:(c + 1) * P].rearrange("p (h d) -> p h d", h=H), ACT.Copy).then_inc(S["v_copied"], 1)

            def attend(s, t):
                if s == "gaff":
                    act.wait_ge(S["affine"], t + 1)
                    sc, bi = gst[:, 5, :], gst[:, 6, :]
                    for k, ps, hi, val in ((0, misc[:, 0:L], q_hi[:, 0:L], e1[:, 0:L]),
                                           (1, misc[:, 256:256 + L], k_hi[:, 0:L], e1[:, LP:LP + L])):
                        for dst in (hi, val):
                            a(dst, ps, ACT.Identity, bias=bi[:, k:k + 1], scale=sc[:, k:k + 1]).then_inc(S["norm"], 1)
                    for b in range(2):
                        a(e2[:, b * L:(b + 1) * L], lg[0][:, b * L:(b + 1) * L], ACT.Identity,
                          bias=bi[:, 2 + b:3 + b], scale=sc[:, 2 + b:3 + b]).then_inc(S["norm"], 1)
                elif s == "vt0":
                    copy_v(0, t)
                elif s == "hkeep":
                    if not is_first(t):
                        act.wait_ge(S["hres_done"], t)
                    a(h2[:, :], h[:, :, :].rearrange("p b l -> p (b l)"), ACT.Copy).then_inc(S["h_kept"], 1)
                elif s == "scores":
                    i = 0
                    for g in range(NG):
                        w = min(OCT, (g + 1) * GRP) - g * GRP
                        for c, (j0, jn) in enumerate(JC):
                            act.wait_ge(S["scores"], t * 14 + i + 1)
                            a(pr[c][0:jn, g * GRP:g * GRP + w, :, :].rearrange("p o b r -> p (o b r)"),
                              lg[(1 + i) % 2][0:jn, 0:w * P], ACT.Exp).then_inc(S["exp_done"], 1)
                            i += 1
                elif s == "pv0":
                    copy_v(1, t)
                elif s == "oaff":
                    act.wait_ge(S["oaffine"], t + 1)
                    for b in range(2):
                        bs = slice(b * L, (b + 1) * L)
                        a(t2[:, bs], t1[:, bs], ACT.Identity, bias=gst_o[:, 6, b:b + 1], scale=gst_o[:, 5, b:b + 1]).then_inc(S["onorm"], 1)
                elif s == "xin":
                    act.wait_ge(S["xp_done"], t + 1)
                    a(x_hi[:, :], V2(t1), ACT.Copy).then_inc(S["xh_done"], 1)

            act.wait_ge(S["setup_dve"], 9)
            act.wait_ge(S["const_in"], N_CONST)
            act.wait_ge(S["w1_in"], 32)
            for piece in range(2):
                a(w1_hi[:, 2048 * piece:2048 * piece + 2048], w1_st[piece], ACT.Copy).then_inc(S["w1_hi_ready"], 1)
            turns(act, attend, mlp, lambda s, n, f: None)

        @block.gpsimd
        def _(pool):
            g = nc.gpsimd

            def gelu_sum(f, n):
                pool.wait_ge(S["g_done"], n * (2 * NF) + 2 * f + 2)
                g.tensor_tensor(gelu1[:, f % RING, :], gelu1[:, f % RING, :], gelu2[:, f % RING, :], ALU.add).then_inc(S["hs_done"], 1)

            def mlp(f, n):
                if f >= SUM_LAG:
                    gelu_sum(f - SUM_LAG, n)

            def end(s, n, f):
                if s == "w2t" and f >= NF - SUM_LAG:
                    gelu_sum(f, n)

            def rsqrt(x, ready, done, t):
                pool.wait_ge(ready, t + 1)
                g.tensor_tensor(x, x, half[0:x.shape[0], 0:1].broadcast_to(list(x.shape)), ALU.pow).then_inc(done, 1)

            def attend(s, t):
                if s in ("var1", "var2"):
                    rsqrt(LN[s[3]][3][0:GW, 0:4], S["vareps" + s[3]], S["rstd" + s[3]], t)
                elif s == "gvar":
                    rsqrt(gst[:, 4, :], S["gve"], S["grstd"], t)
                elif s == "ovar":
                    rsqrt(gst_o[:, 4, 0:2], S["ove"], S["orstd"], t)
                elif s[:2] == "qs":
                    k, part = divmod(int(s[2]), 2)
                    x = (q_hi, q_lo)[k]
                    if k == 0:
                        pool.wait_ge(S["norm"], t * 6 + 4)
                    else:
                        pool.wait_ge(S["lo"], t * 2 + 2)
                    o0, on = ((0, 13), (13, OCT - 13))[part]
                    g.tensor_tensor(q_bd[k][:, o0:o0 + on, :, :],
                                    x[:, 8 * o0:8 * (o0 + on)].bitcast(F32).rearrange("p (o r) -> p o r", r=8).unsqueeze(2).broadcast_to([P, on, BH, 8]),
                                    K["mask_bh"].unsqueeze(1).unsqueeze(3).broadcast_to([P, on, BH, 8]), ALU.mult).then_inc(S["q_spread"], 1)
                elif s == "gate":
                    pool.wait_ge(S["dl_ready"], t + 1)
                    g.tensor_tensor(ep[0:GW, 0:4], half[0:GW, 1:2].broadcast_to([GW, 4]), dl[0:GW, 0:4], ALU.pow).then_inc(S["e_ready"], 1)

            pool.wait_ge(S["setup_dve"], 9)
            pool.wait_ge(S["const_in"], N_CONST)
            turns(pool, attend, mlp, end)


def build(nc, a, out):
    tok_scratch = nc.dram_tensor("tok_scratch", (P, B, NPATCH), F32, kind="Internal").ap()
    with ExitStack() as ctx:
        R = resident(nc, ctx)
        patch_embed(nc, a, tok_scratch, R)
        fused_block(nc, a["txt"], a["w1"], tok_scratch, out.rearrange("b l c -> (b l) c"), R)


def shape_constants(np):
    c = np.zeros((P, NCONST), np.float32)
    p = np.arange(P)

    def put(name, value):
        a, w = CO[name]
        c[:, a:a + w] = value

    put("ident", np.eye(P))
    put("ones", 1.0 / P)
    put("g8", (p[:, None] // 8 == p[None] // 8) / 8.0)
    put("g4", (p[:, None] // 4 == p[None] // 4) / 4.0)
    put("mask_bh", p[:, None] // DK == np.arange(BH)[None])
    put("mask_r", p[:, None] // HD == np.arange(8)[None])
    put("mask_q", p[:, None] % 8 == np.arange(8)[None])
    w = np.zeros((P, 112 + HD + 112))
    w[:, 112:112 + HD] = p[:, None] % HD == np.arange(HD)[None]
    put("place", w)
    return c


def kernel(**inputs):
    import numpy as np
    import concourse.bacc as bacc
    from concourse.bass_utils import run_bass_kernel_spmd

    i = {k: np.asarray(v) for k, v in inputs.items()}
    qkv = i["L0_attn_W_qkv"].reshape(P, H, 2 * HD)
    parts = (slice(0, DK), slice(DK, 2 * DK), slice(2 * DK, 2 * HD))

    def gn_columns(v):
        q, k, val = (v.reshape(H, 2 * HD)[:, s].reshape(-1) for s in parts)
        return [np.concatenate([q, q]), np.concatenate([k, k]), val, val]

    rel = i["L0_attn_rel_emb"]
    arrays = {
        "x": i["x"], "txt": i["txt"],
        "w_tok": i["L0_tok_W"].reshape(P, ROWS, PATCH).transpose(1, 2, 0),
        "b_tok": i["L0_tok_b"].reshape(P, 1), "cls": i["L0_tok_class_token"].reshape(P, 1),
        "pos": i["L0_tok_pos_embed"].T,
        "wq": qkv[:, :, parts[0]].reshape(P, -1), "wk": qkv[:, :, parts[1]].reshape(P, -1), "wv": qkv[:, :, parts[2]].reshape(P, -1),
        "gn_in": np.stack(gn_columns(i["L0_attn_gn_qkv_scale"]) + gn_columns(i["L0_attn_gn_qkv_bias"]), 1),
        "rel_rev": rel[0:HD, ::-1], "rel_v": rel[HD:2 * HD].T[np.maximum(np.arange(LP + P)[None] - np.arange(P)[:, None] + 64, 0)].reshape(P, -1),
        "gn_out": np.stack([i["L0_attn_gn_out_scale"], i["L0_attn_gn_out_bias"]], 1),
        "wg": i["L0_ffn_Wg"], "w1": i["L0_ffn_W1"], "b1": i["L0_ffn_b1"].reshape(NF, P).T,
        "w2": i["L0_ffn_W2"].reshape(NF, P, P).transpose(1, 0, 2), "b2": i["L0_ffn_b2"].T,
        "consts": shape_constants(np),
    }
    arrays = {f"in_{k}": np.ascontiguousarray(v) for k, v in arrays.items()}
    nc = bacc.Bacc("TRN2", target_bir_lowering=False, num_devices=1)
    aps = {k[3:]: nc.dram_tensor(k, v.shape, mybir.dt.from_np(v.dtype), kind="ExternalInput").ap() for k, v in arrays.items()}
    out = nc.dram_tensor("out", (B, L, P), F32, kind="ExternalOutput").ap()
    build(nc, aps, out)
    return run_bass_kernel_spmd(nc, [arrays], core_ids=[0]).results[0]["out"]
```
